# Optimizing a Trainium2 kernel written in Bass

```python
import numpy as np
import jax
import jax.numpy as jnp

def _softmax(x, axis=-1):
    return jax.nn.softmax(x, axis=axis)

def _gelu(x):
    return jax.nn.gelu(x, approximate=True)

def _silu(x):
    return jax.nn.silu(x)

def _sigmoid(x):
    return jax.nn.sigmoid(x)

def _layernorm(x, axis=-1, eps=1e-05):
    m = jnp.mean(x, axis=axis, keepdims=True)
    v = jnp.var(x, axis=axis, keepdims=True)
    return (x - m) / jnp.sqrt(v + eps)

def _scatter_add(tgt, idx, src, axis=0):
    return tgt.at[idx].add(src)

def _segment_sum(src, seg, n):
    return jax.ops.segment_sum(src, seg, n)
kernel_name = 'mk_gnn_resnorm_d4_gnn_r8_927f0b'

def setup_inputs(seed: int=0):
    np.random.seed(seed)
    _w = jnp.asarray

    def _rec_inputs():
        import jax
        import jax.numpy as jnp
        _gk = jax.random.key(seed)
        x = -0.000202 + 1 * jax.random.normal(jax.random.fold_in(_gk, 1), (12500, 64), jnp.float32)
        src = jax.random.randint(jax.random.fold_in(_gk, 2), (200000,), 0, 12500, jnp.int32)
        dst = jnp.minimum((12500 * jax.random.uniform(jax.random.fold_in(_gk, 3), (200000,)) ** 2.0).astype(jnp.int32), 99999)
        _o = jnp.argsort(dst, stable=True)
        src = src[_o]
        dst = dst[_o]
        edge_attr_64 = -6.74381e-05 + 0.999835 * jax.random.normal(jax.random.fold_in(_gk, 12), (200000, 64), jnp.float32)
        return (x, src, dst, edge_attr_64)
    x, src, dst, edge_attr_64 = _rec_inputs()

    def _L0_gnn_setup():
        import jax, jax.numpy as jnp
        import numpy as np
        N = 12500
        E = 200000
        D = 64
        H = 4
        NEG_SLOPE = 0.2
        key = jax.random.key(seed)
        ks = jax.random.split(key, 8)
        x = jax.random.normal(ks[0], (N, D), dtype=jnp.float32)
        edge_index = jax.random.randint(ks[1], (2, E), 0, N, dtype=jnp.int64)
        s = 1.0 / np.sqrt(D)
        W = jax.random.uniform(ks[2], (D, H * D), jnp.float32, -s, s)
        att_src = jax.random.uniform(ks[3], (H, D), jnp.float32, -s, s)
        att_dst = jax.random.uniform(ks[4], (H, D), jnp.float32, -s, s)
        bias = jnp.zeros((H * D,), jnp.float32)
        s2 = 1.0 / np.sqrt(H * D)
        Wl = jax.random.uniform(ks[5], (H * D, D), jnp.float32, -s2, s2)
        bl = jax.random.uniform(ks[6], (D,), jnp.float32, -s2, s2)
        return {'x': x, 'edge_index': edge_index, 'W': W, 'att_src': att_src, 'att_dst': att_dst, 'bias': bias, 'Wl': Wl, 'bl': bl}
    _L0_gnn_all = _L0_gnn_setup()
    _L0_gnn_in = {k: v for k, v in _L0_gnn_all.items() if k in ('W', 'att_src', 'att_dst', 'bias', 'Wl', 'bl')}
    del _L0_gnn_all

    def _L1_gnn_setup():
        import jax, jax.numpy as jnp
        import numpy as np
        N_NODES = 12500
        N_EDGES = 200000
        N_FEAT = 64
        EPS = 1e-08
        key = jax.random.key(seed)
        kx, ke = jax.random.split(key)
        x = jax.random.normal(kx, (N_NODES, N_FEAT), dtype=jnp.float32)
        edge_index = jax.random.randint(ke, (2, N_EDGES), 0, N_NODES, dtype=jnp.int32)
        return {'x': x, 'edge_index': edge_index}
    _L1_gnn_all = _L1_gnn_setup()
    _L1_gnn_in = {k: v for k, v in _L1_gnn_all.items() if k in ()}
    del _L1_gnn_all

    def _L2_gnn_setup():
        import jax, jax.numpy as jnp
        import numpy as np
        N_NODES = 12500
        N_EDGES = 156250
        D = 64
        H = 128
        key = jax.random.key(seed)
        ks = jax.random.split(key, 8)
        s = 1.0 / np.sqrt(D)
        return {'nodes': jax.random.normal(ks[0], (N_NODES, D), jnp.float32), 'edges': jax.random.normal(ks[1], (N_EDGES, D), jnp.float32), 'senders': jax.random.randint(ks[2], (N_EDGES,), 0, N_NODES, jnp.int32), 'receivers': jax.random.randint(ks[3], (N_EDGES,), 0, N_NODES, jnp.int32), 'We_w': jax.random.normal(ks[4], (D, D), jnp.float32) * s, 'We_b': jnp.zeros((D,), jnp.float32), 'eps': jnp.zeros((1, 1), jnp.float32), 'W1': jax.random.normal(ks[5], (D, H), jnp.float32) * s, 'b1': jnp.zeros((H,), jnp.float32), 'W2': jax.random.normal(ks[6], (H, D), jnp.float32) * (1.0 / np.sqrt(H)), 'b2': jnp.zeros((D,), jnp.float32)}
    _L2_gnn_all = _L2_gnn_setup()
    _L2_gnn_in = {k: v for k, v in _L2_gnn_all.items() if k in ('We_w', 'We_b', 'eps', 'W1', 'b1', 'W2', 'b2')}
    del _L2_gnn_all

    def _L3_gnn_setup():
        import jax, jax.numpy as jnp
        import numpy as np
        N_NODES = 12500

        def sage_conv(x, src, dst, Wl, bl, Wr):
            msg = x[src]
            agg = jax.ops.segment_sum(msg, dst, num_segments=N_NODES)
            deg = jax.ops.segment_sum(jnp.ones((src.shape[0], 1), x.dtype), dst, num_segments=N_NODES)
            agg = agg / jnp.maximum(deg, 1.0)
            return agg @ Wl.T + bl + x @ Wr.T
        key = jax.random.key(seed)
        ks = jax.random.split(key, 16)
        in_d, hid, lat = (64, 128, 32)
        x = jax.random.normal(ks[0], (N_NODES, in_d), dtype=jnp.float32)
        edge_index = jax.random.randint(ks[1], (2, 200000), 0, N_NODES, dtype=jnp.int64)

        def lin(k, out_d, inp_d):
            s = 1.0 / np.sqrt(inp_d)
            return jax.random.uniform(k, (out_d, inp_d), jnp.float32, -s, s)
        dims = [(hid, in_d), (lat, hid), (hid, lat), (in_d, hid)]
        inp = {'x': x, 'edge_index': edge_index}
        for i, (o, c) in enumerate(dims, start=1):
            inp[f'Wl{i}'] = lin(ks[2 + 3 * (i - 1)], o, c)
            inp[f'bl{i}'] = jnp.zeros((o,), jnp.float32)
            inp[f'Wr{i}'] = lin(ks[3 + 3 * (i - 1)], o, c)
        return inp
    _L3_gnn_all = _L3_gnn_setup()
    _L3_gnn_in = {k: v for k, v in _L3_gnn_all.items() if k in ('Wl1', 'bl1', 'Wr1', 'Wl2', 'bl2', 'Wr2', 'Wl3', 'bl3', 'Wr3', 'Wl4', 'bl4', 'Wr4')}
    del _L3_gnn_all
    return {'x': x, 'src': src, 'dst': dst, 'edge_attr_64': edge_attr_64, 'L0_gnn_W': _L0_gnn_in['W'], 'L0_gnn_att_src': _L0_gnn_in['att_src'], 'L0_gnn_att_dst': _L0_gnn_in['att_dst'], 'L0_gnn_bias': _L0_gnn_in['bias'], 'L0_gnn_Wl': _L0_gnn_in['Wl'], 'L0_gnn_bl': _L0_gnn_in['bl'], 'L2_gnn_We_w': _L2_gnn_in['We_w'], 'L2_gnn_We_b': _L2_gnn_in['We_b'], 'L2_gnn_eps': _L2_gnn_in['eps'], 'L2_gnn_W1': _L2_gnn_in['W1'], 'L2_gnn_b1': _L2_gnn_in['b1'], 'L2_gnn_W2': _L2_gnn_in['W2'], 'L2_gnn_b2': _L2_gnn_in['b2'], 'L3_gnn_Wl1': _L3_gnn_in['Wl1'], 'L3_gnn_bl1': _L3_gnn_in['bl1'], 'L3_gnn_Wr1': _L3_gnn_in['Wr1'], 'L3_gnn_Wl2': _L3_gnn_in['Wl2'], 'L3_gnn_bl2': _L3_gnn_in['bl2'], 'L3_gnn_Wr2': _L3_gnn_in['Wr2'], 'L3_gnn_Wl3': _L3_gnn_in['Wl3'], 'L3_gnn_bl3': _L3_gnn_in['bl3'], 'L3_gnn_Wr3': _L3_gnn_in['Wr3'], 'L3_gnn_Wl4': _L3_gnn_in['Wl4'], 'L3_gnn_bl4': _L3_gnn_in['bl4'], 'L3_gnn_Wr4': _L3_gnn_in['Wr4']}

def reference(x, src, dst, edge_attr_64, L0_gnn_W, L0_gnn_att_src, L0_gnn_att_dst, L0_gnn_bias, L0_gnn_Wl, L0_gnn_bl, L2_gnn_We_w, L2_gnn_We_b, L2_gnn_eps, L2_gnn_W1, L2_gnn_b1, L2_gnn_W2, L2_gnn_b2, L3_gnn_Wl1, L3_gnn_bl1, L3_gnn_Wr1, L3_gnn_Wl2, L3_gnn_bl2, L3_gnn_Wr2, L3_gnn_Wl3, L3_gnn_bl3, L3_gnn_Wr3, L3_gnn_Wl4, L3_gnn_bl4, L3_gnn_Wr4):
    import jax
    import jax.numpy as jnp

    def _L0_gnn_ref(x, edge_index, W, att_src, att_dst, bias, Wl, bl):
        import jax, jax.numpy as jnp
        import numpy as np
        N = 12500
        E = 200000
        D = 64
        H = 4
        NEG_SLOPE = 0.2
        h = (x @ W).reshape(N, H, D)
        loop = jnp.arange(N, dtype=edge_index.dtype)
        src = jnp.concatenate([edge_index[0], loop])
        dst = jnp.concatenate([edge_index[1], loop])
        a_src = jnp.einsum('nhd,hd->nh', h, att_src)
        a_dst = jnp.einsum('nhd,hd->nh', h, att_dst)
        alpha = a_src[src] + a_dst[dst]
        alpha = jax.nn.leaky_relu(alpha, NEG_SLOPE)
        amax = jax.ops.segment_max(alpha, dst, num_segments=N)
        alpha = jnp.exp(alpha - jax.lax.stop_gradient(amax)[dst])
        denom = jax.ops.segment_sum(alpha, dst, num_segments=N)
        alpha = alpha / (denom[dst] + 1e-16)
        msg = h[src] * alpha[:, :, None]
        out = jax.ops.segment_sum(msg, dst, num_segments=N)
        out = out.reshape(N, H * D) + bias
        return out @ Wl + bl

    def _L1_gnn_ref(x, edge_index):
        import jax, jax.numpy as jnp
        import numpy as np
        N_NODES = 12500
        N_EDGES = 200000
        N_FEAT = 64
        EPS = 1e-08
        src = edge_index[0]
        tgt = edge_index[1]
        num_nodes = x.shape[0]
        messages = jnp.take(x, src, axis=0)
        ones = jnp.ones((messages.shape[0], 1), dtype=messages.dtype)
        count = jax.ops.segment_sum(ones, tgt, num_segments=num_nodes)
        sum_msgs = jax.ops.segment_sum(messages, tgt, num_segments=num_nodes)
        safe_count = jnp.maximum(count, jnp.asarray(EPS, dtype=count.dtype))
        mean = sum_msgs / safe_count
        mean_per_edge = jnp.take(mean, tgt, axis=0)
        squared_diff = jnp.square(messages - mean_per_edge)
        sum_sq = jax.ops.segment_sum(squared_diff, tgt, num_segments=num_nodes)
        variance = sum_sq / safe_count
        std_dev = jnp.sqrt(jnp.maximum(variance, jnp.zeros_like(variance)))
        std_dev = jnp.where(count <= 1, jnp.zeros_like(std_dev), std_dev)
        return std_dev

    def _L2_gnn_ref(nodes, edges, senders, receivers, We_w, We_b, eps, W1, b1, W2, b2):
        import jax, jax.numpy as jnp
        import numpy as np
        N_NODES = 12500
        N_EDGES = 156250
        D = 64
        H = 128
        msg = nodes[senders] + (edges @ We_w + We_b)
        agg = jax.ops.segment_sum(msg, receivers, num_segments=N_NODES)
        h = (1.0 + eps) * nodes + agg
        h = jax.nn.relu(h @ W1 + b1)
        out = h @ W2 + b2
        return out

    def _L3_gnn_ref(x, edge_index, Wl1, bl1, Wr1, Wl2, bl2, Wr2, Wl3, bl3, Wr3, Wl4, bl4, Wr4):
        import jax, jax.numpy as jnp
        import numpy as np
        N_NODES = 12500

        def sage_conv(x, src, dst, Wl, bl, Wr):
            msg = x[src]
            agg = jax.ops.segment_sum(msg, dst, num_segments=N_NODES)
            deg = jax.ops.segment_sum(jnp.ones((src.shape[0], 1), x.dtype), dst, num_segments=N_NODES)
            agg = agg / jnp.maximum(deg, 1.0)
            return agg @ Wl.T + bl + x @ Wr.T
        src, dst = (edge_index[0], edge_index[1])
        h = jax.nn.relu(sage_conv(x, src, dst, Wl1, bl1, Wr1))
        z = sage_conv(h, src, dst, Wl2, bl2, Wr2)
        h = jax.nn.relu(sage_conv(z, src, dst, Wl3, bl3, Wr3))
        x_hat = sage_conv(h, src, dst, Wl4, bl4, Wr4)
        return x_hat
    edge_index = jnp.stack([src, dst])
    x = _layernorm(x + _L0_gnn_ref(x, edge_index, L0_gnn_W, L0_gnn_att_src, L0_gnn_att_dst, L0_gnn_bias, L0_gnn_Wl, L0_gnn_bl), axis=-1)
    x = _layernorm(x + _L1_gnn_ref(x, edge_index), axis=-1)
    x = _layernorm(x + _L2_gnn_ref(x, edge_attr_64, src, dst, L2_gnn_We_w, L2_gnn_We_b, L2_gnn_eps, L2_gnn_W1, L2_gnn_b1, L2_gnn_W2, L2_gnn_b2), axis=-1)
    x = _layernorm(x + _L3_gnn_ref(x, edge_index, L3_gnn_Wl1, L3_gnn_bl1, L3_gnn_Wr1, L3_gnn_Wl2, L3_gnn_bl2, L3_gnn_Wr2, L3_gnn_Wl3, L3_gnn_bl3, L3_gnn_Wr3, L3_gnn_Wl4, L3_gnn_bl4, L3_gnn_Wr4), axis=-1)
    return x

_drawn_inputs = setup_inputs


def setup_inputs(seed=0):
    import zlib

    import numpy as np

    out = dict(_drawn_inputs(seed))
    spreads = {'L0_gnn_bias': (0.0, 0.1),
     'L2_gnn_We_b': (0.0, 0.1),
     'L2_gnn_b1': (0.0, 0.424),
     'L2_gnn_b2': (0.0, 0.3),
     'L3_gnn_bl1': (0.0, 0.34),
     'L3_gnn_bl2': (0.0, 0.1),
     'L3_gnn_bl3': (0.0, 0.1),
     'L3_gnn_bl4': (0.0, 0.1)}
    factors = {'L0_gnn_att_dst': 8.0}
    for name, (base, spread) in spreads.items():
        noise = np.random.default_rng([zlib.crc32(name.encode()), seed]).standard_normal(out[name].shape)
        drawn = base * np.exp(spread * noise) if base else spread * noise
        out[name] = jnp.asarray(drawn.astype(out[name].dtype))
    for name, factor in factors.items():
        out[name] = (out[name] * factor).astype(out[name].dtype)
    return out
```

```python
import math
from contextlib import ExitStack

import concourse.bass as bass
from concourse import mybir

F32 = mybir.dt.float32
BF16 = mybir.dt.bfloat16
I32 = mybir.dt.int32
ALU = mybir.AluOpType
ACT = mybir.ActivationFunctionType
X_AXIS = mybir.AxisListType.X

P = 128
N_NODES = 12500
N_EDGES = 200000
D = 64
H = 4
HID = 128
LAT = 32
TILES = -(-N_NODES // P)
TAIL = N_NODES - (TILES - 1) * P
NPAD = TILES * P
C = 4
GE = P * C
SLOTS = 4
ROUNDS = -(-N_EDGES // (GE * SLOTS))
GROUPS = ROUNDS * SLOTS
FULL_GROUPS = N_EDGES // GE
EDGE_TAIL_P = (N_EDGES - FULL_GROUPS * GE) // C
TB = 7
BLOCKS = TILES // TB
HALF = TB * P // 2
NEG_SLOPE = 0.2
LN_EPS = 1e-5
GATW = H * D + H + 1
GAT_ROW = D + H
assert BLOCKS * TB == TILES and (N_EDGES - FULL_GROUPS * GE) % C == 0


class Chain:

    def __init__(self, eng, sem):
        self.eng, self.sem, self.base, self.it, self.per, self.n = eng, sem, 0, 0, 0, 0

    def loop(self, it, per):
        if self.per == 0:
            self.base += self.n
        self.it, self.per, self.n = it, per, 0

    def __call__(self, ins):
        self.n += 1
        ins.then_inc(self.sem, 1)
        self.eng.wait_ge(self.sem, (self.base + self.n) if self.per == 0 else self.it * self.per + (self.base + self.n))

    def close(self, trips):
        assert self.n == self.per, (self.n, self.per)
        self.base += trips * self.per
        self.it, self.per, self.n = 0, 0, 0


def build(nc, x, edge_attr, src_r, dst_r, dst_b, w, out):
    ctx = ExitStack()
    with ctx:
        def sb(name, shape, dt=F32):
            return ctx.enter_context(nc.sbuf_tensor(name, shape, dt))

        def sem(name):
            return ctx.enter_context(nc.semaphore(name))

        passes = [
            dict(name="gat", parts=1, n=GATW, row=GAT_ROW),
            dict(name="dev", parts=3, n=2 * D, row=6 * D),
            dict(name="gine", parts=1, n=2 * D, row=D),
            dict(name="sage1", parts=3, n=D, row=3 * D),
            dict(name="sage2", parts=3, n=LAT, row=3 * LAT),
            dict(name="sage3", parts=3, n=LAT, row=3 * LAT),
            dict(name="sage4", parts=3, n=D, row=3 * D),
        ]
        for ps in passes:
            dt = F32 if ps["parts"] == 1 else BF16
            ps["dt"] = dt
            ps["table"] = nc.dram_tensor(f"table_{ps['name']}", (NPAD, ps["row"]), dt, kind="Internal").ap()
            ps["table_tiles"] = ps["table"].rearrange("(t p) w -> p t w", p=P)
            ps["table_done"] = sem(f"table_done_{ps['name']}")
            ps["gathered"] = [sem(f"gathered_{ps['name']}_{s}") for s in range(SLOTS)]
            ps["onehot_ready"] = sem(f"onehot_ready_{ps['name']}")
            ps["agg_done"] = sem(f"agg_done_{ps['name']}")
            ps["acc_done"] = sem(f"acc_done_{ps['name']}")
        mlp, norm = ["gine", "sage1", "sage3"], ["gat", "dev", "gine", "sage4"]
        step_users = {"stack_ready": ["gat"] + mlp, "turned": ["gat"] + mlp, "copied": ["gat"] + mlp, "hidden": mlp,
                      "relued": mlp, "product": ["gat"] + mlp, "var_ready": norm, "std_ready": norm}
        step_sem = {key: sem(key) for key in step_users}

        def block_count(key, name, b):
            return b + (step_users[key].index(name) * BLOCKS + 1)

        idx_loaded = [sem(f"idx_loaded_{s}") for s in range(SLOTS)]
        slots_free = sem("slots_free")
        dstb_loaded = [sem(f"dstb_loaded_{s}") for s in range(SLOTS)]
        edges_loaded = [sem(f"edges_loaded_{s}") for s in range(SLOTS)]
        nodehot_ready, expand_done, expand_open = sem("nodehot_ready"), sem("expand_done"), sem("expand_open")
        logit_ready, weight_ready = sem("logit_ready"), sem("weight_ready")
        loaded, consts_ready, x_loaded = sem("loaded"), sem("consts_ready"), sem("x_loaded")
        x_zeroed = sem("x_zeroed")
        prep_v, prep_t, span_in, span_red = sem("prep_v"), sem("prep_t"), sem("span_in"), sem("span_red")
        prep_done, score_t, score_c, score_m = sem("prep_done"), sem("score_t"), sem("score_c"), sem("score_m")
        range_in, range_red, self_in, self_exp = sem("range_in"), sem("range_red"), sem("self_in"), sem("self_exp")
        chain_sem = sem("vector_step")
        out_done = sem("out_done")
        waits_passed = sem("waits_passed")
        score_mm, score_in = sem("score_mm"), sem("score_in")
        dev_in, dev_out = sem("dev_in"), sem("dev_out")
        pass_open = sem("pass_open")
        rows_ready = [None] + [sem(f"rows_ready_{k}") for k in range(1, len(passes) + 1)]

        X = sb("X", [P, TILES, D])
        ACC = sb("ACC", [P, TILES * GATW])
        DEG = sb("DEG", [P, TILES])
        RDEG = sb("RDEG", [P, TILES])
        DST = sb("DST", [P, GROUPS * C])
        NODE = sb("NODE", [P, TILES])
        TBASE = sb("TBASE", [P, TILES])
        COL = sb("COL", [P, P])
        IDENT = sb("IDENT", [P, P])
        ZERO = sb("ZERO", [P, P], BF16)
        span = sb("span", [P, 2, GROUPS])
        SPAN = sb("SPAN", [P, GROUPS, 2], I32)
        idx = sb("idx", [P, SLOTS, C], I32)
        dstb = sb("dstb", [P, SLOTS, GE], I32)
        gathered = sb("gathered", [P, SLOTS * C * 3 * D])
        gf = gathered[:, 0:SLOTS * C * 2 * D].rearrange("p (s c w) -> p s c w", s=SLOTS, c=C)
        gh = gathered[:, :].bitcast(BF16).rearrange("p (s c w) -> p s c w", s=SLOTS, c=C)
        onehot = sb("onehot", [P, C, P])
        onehot_h = sb("onehot_h", [P, C, P], BF16)
        nodehot = sb("nodehot", [P, GE], BF16)
        msg = sb("msg", [P, C, GATW])
        wts = sb("wts", [P, C, H])
        lg = sb("lg", [P, 3, C, H])
        VALS = sb("VALS", [P, TILES, 3, 2 * H], BF16)
        ASRC = sb("ASRC", [P, TILES, 2 * H])
        WSELF = sb("WSELF", [P, TILES, H])
        rangev = sb("rangev", [P, 2 * H])
        big = sb("big", [P, TB * H * D])
        dst_i = big[:, 0:GROUPS * C].bitcast(I32)
        bigT = sb("bigT", [P, TB * H * D])
        rows = dstb[:, :, :].rearrange("p s e -> p (s e)").bitcast(BF16)[:, 0:TB * 6 * D]
        tmp = sb("tmp", [P, 4, TB * D])
        score_rows = tmp[:, :, :].rearrange("p a k -> p (a k)")[:, 0:TB * GAT_ROW]
        small = sb("small", [P, 8, TILES])
        used = [0]

        def early(rows, cols):
            at = used[0]
            used[0] += cols
            return ACC[0:rows, at:at + cols]

        W = early(D, H * D)
        att = early(D, 2 * H * D).rearrange("p (a k) -> p a k", a=2)
        biasc = early(P, 2)
        biasb = early(P, 2 * P).rearrange("p (a k) -> p a k", a=2)
        BD = early(P, 2 * P).rearrange("p (a k) -> p a k", a=2)
        bl = early(P, D)
        WeT = early(D, 2 * D).rearrange("p (a k) -> p a k", a=2)
        We = early(D, D)
        W1 = early(D, HID)
        nat1, nat2 = early(HID, 2 * D), early(2 * LAT, HID)
        nat3, nat4 = early(HID, 2 * LAT), early(2 * D, HID)
        Wl = early(P, 2 * D).rearrange("p (a k) -> p a k", a=2)
        Wa = sb("Wa", [D, 2 * H])
        MST = sb("MST", [P, 2, D])
        CV = sb("CV", [P, D])
        Web = sb("Web", [P, D])
        epsb = sb("epsb", [P, 1])
        W1S = sb("W1S", [P, HID])
        b1 = sb("b1", [P, 1])
        W2 = sb("W2", [P, D])
        b2 = sb("b2", [P, D])
        S1, S2 = sb("S1", [P, HID]), sb("S2", [HID, 2 * LAT])
        S3, S4 = sb("S3", [2 * LAT, HID]), sb("S4", [HID, 2 * D])
        sb1, sb2 = sb("sb1", [P, 1]), sb("sb2", [P, LAT])
        sb3, sb4 = sb("sb3", [P, 1]), sb("sb4", [P, D])
        hid = bigT[:, TB * P:2 * TB * P]

        def psum(name, cols):
            return ctx.enter_context(nc.psum_tensor(name, [P, cols], F32))

        ps_turn = psum("ps_turn", 2048)
        ps_hid = psum("ps_hid", 1024)
        ps_out = psum("ps_out", 1024)
        ps_agg = ps_out[:, 0:512]
        ps_exp = ps_hid[:, 0:C * 2 * H].rearrange("p (c k) -> p c k", c=C)

        def flat(lo, n, cols):
            return ACC[:, lo * TILES:lo * TILES + TILES * cols].rearrange("p (t k) -> p t k", k=cols)

        acc_of = [flat(0, 0, ps["n"]) for ps in passes]
        Q2, Z, Q4 = flat(64, 0, LAT), flat(96, 0, LAT), flat(128, 0, D)

        const_loads = [
            (W[:, :], w["L0_gnn_W"]),
            (att[:, 0, :], w["L0_gnn_att_src"].rearrange("h d -> (h d)").partition_broadcast(D)),
            (att[:, 1, :], w["L0_gnn_att_dst"].rearrange("h d -> (h d)").partition_broadcast(D)),
            (Wl[:, :, :], w["L0_gnn_Wl"].rearrange("(k p) n -> p k n", p=P)),
            (biasc[:, 0:1], w["L0_gnn_bias"][0:P].rearrange("(p a) -> p a", a=1)),
            (biasc[:, 1:2], w["L0_gnn_bias"][P:2 * P].rearrange("(p a) -> p a", a=1)),
            (bl[:, :], w["L0_gnn_bl"].partition_broadcast(P)),
            (We[:, :], w["L2_gnn_We_w"]),
            (Web[:, :], w["L2_gnn_We_b"].partition_broadcast(P)),
            (epsb[:, :], w["L2_gnn_eps"].rearrange("a b -> (a b)").partition_broadcast(P)),
            (W1[:, :], w["L2_gnn_W1"]),
            (b1[:, :], w["L2_gnn_b1"].rearrange("(p a) -> p a", a=1)),
            (W2[:, :], w["L2_gnn_W2"]),
            (b2[:, :], w["L2_gnn_b2"].partition_broadcast(P)),
            (nat1[:, 0:D], w["L3_gnn_Wl1"]), (nat1[:, D:2 * D], w["L3_gnn_Wr1"]),
            (nat2[0:LAT, :], w["L3_gnn_Wl2"]), (nat2[LAT:2 * LAT, :], w["L3_gnn_Wr2"]),
            (nat3[:, 0:LAT], w["L3_gnn_Wl3"]), (nat3[:, LAT:2 * LAT], w["L3_gnn_Wr3"]),
            (nat4[0:D, :], w["L3_gnn_Wl4"]), (nat4[D:2 * D, :], w["L3_gnn_Wr4"]),
            (sb1[:, :], w["L3_gnn_bl1"].rearrange("(p a) -> p a", a=1)),
            (sb2[:, :], w["L3_gnn_bl2"].partition_broadcast(P)),
            (sb3[:, :], w["L3_gnn_bl3"].rearrange("(p a) -> p a", a=1)),
            (sb4[:, :], w["L3_gnn_bl4"].partition_broadcast(P)),
            (dst_i, dst_r),
        ]
        N_CONST = 16 * len(const_loads)
        N_X = 16 * 2
        block = ctx.enter_context(nc.Block())

        def settle(eng):
            eng.sem_inc(waits_passed, 1)

        def span_of(eng, regs, g):
            eng.reg_load(regs, SPAN[0:1, bass.ds(g, 1), :].rearrange("p a b -> p (a b)"))
            return (eng.snap(regs[0], min_val=0, max_val=TILES - 1), eng.snap(regs[1], min_val=1, max_val=TILES))

        @block.sync
        def _(sp):
            for dst, src in const_loads:
                sp.dma_start(dst, src).then_inc(loaded, 16)
            sp.dma_start(X[:, 0:TILES - 1, :], x[0:(TILES - 1) * P, :].rearrange("(t p) d -> p t d", p=P)).then_inc(x_loaded, 16)
            sp.wait_ge(x_zeroed, 1)
            sp.dma_start(X[0:TAIL, TILES - 1, :], x[(TILES - 1) * P:N_NODES, :]).then_inc(x_loaded, 16)

            def store_table(k, ready, source):
                ps = passes[k]
                with sp.Fori(0, BLOCKS) as b:
                    sp.wait_ge(ready, b + 1)
                    sp.dma_start(ps["table_tiles"][:, bass.ds(b * TB, TB), :], source(b)).then_inc(ps["table_done"], 16)

            def feed(k):
                ps = passes[k]

                def one(i, s, edges):
                    g = i * SLOTS + s
                    sp.wait_ge(ps["gathered"][s], i * (16 * C))
                    sp.dma_start(idx[:, s, :], src_r[:, bass.ds(g * C, C)] if not isinstance(g, int) else src_r[:, g * C:(g + 1) * C]).then_inc(idx_loaded[s], 16)
                    if ps["name"] == "gat":
                        sp.wait_ge(slots_free, g + (k * GROUPS + 1))
                        sp.dma_start(dstb[:, s, :], dst_b[bass.ds(g, 1), :].rearrange("a e -> (a e)").partition_broadcast(P)).then_inc(dstb_loaded[s], 16)
                    if ps["name"] == "gine":
                        sp.wait_ge(slots_free, g + (k * GROUPS + 1))
                        if not edges:
                            sp.sem_inc(edges_loaded[s], 16)
                        else:
                            e = edge_attr[bass.ds(g * GE, edges * C), :] if not isinstance(g, int) else edge_attr[g * GE:g * GE + edges * C, :]
                            sp.dma_start(gf[0:edges, s, :, D:2 * D], e.rearrange("(p c) d -> p c d", c=C)).then_inc(edges_loaded[s], 16)

                if ps["name"] != "gine":
                    with sp.Fori(0, ROUNDS) as i:
                        for s in range(SLOTS):
                            one(i, s, P)
                else:
                    with sp.Fori(0, ROUNDS - 1) as i:
                        for s in range(SLOTS):
                            one(i, s, P)
                    for s in range(SLOTS):
                        g = (ROUNDS - 1) * SLOTS + s
                        one(ROUNDS - 1, s, P if g < FULL_GROUPS else EDGE_TAIL_P if g == FULL_GROUPS else 0)

            store_table(0, score_m, lambda b: score_rows.rearrange("p (t k) -> p t k", t=TB))
            for k, ps in enumerate(passes):
                feed(k)
                if k + 1 < len(passes):
                    nxt = passes[k + 1]
                    if nxt["name"] == "gine":
                        store_table(k + 1, rows_ready[k + 1], lambda b: X[:, bass.ds(b * TB, TB), :])
                    else:
                        store_table(k + 1, rows_ready[k + 1],
                                    lambda b, r=nxt["row"]: rows[:, 0:TB * r].rearrange("p (t k) -> p t k", t=TB))
                else:
                    with sp.Fori(0, BLOCKS - 1) as b:
                        sp.wait_ge(rows_ready[k + 1], b + 1)
                        sp.dma_start(out[bass.ds(b * (TB * P), TB * P), :].rearrange("(t p) d -> p t d", p=P),
                                     X[:, bass.ds(b * TB, TB), :]).then_inc(out_done, 16)
                    sp.wait_ge(rows_ready[k + 1], BLOCKS)
                    first = (BLOCKS - 1) * TB
                    sp.dma_start(out[first * P:(TILES - 1) * P, :].rearrange("(t p) d -> p t d", p=P),
                                 X[:, first:TILES - 1, :]).then_inc(out_done, 16)
                    sp.dma_start(out[(TILES - 1) * P:N_NODES, :], X[0:TAIL, TILES - 1, :]).then_inc(out_done, 16)
            sp.wait_ge(out_done, 16 * (BLOCKS + 1))

        @block.gpsimd
        def _(pool):
            pool.iota(COL[:, :], [[1, P]], base=0, channel_multiplier=0, allow_small_or_imprecise_dtypes=True).then_inc(consts_ready, 1)
            pool.iota(TBASE[:, :], [[P, TILES]], base=0, channel_multiplier=0, allow_small_or_imprecise_dtypes=True).then_inc(consts_ready, 1)
            pool.iota(NODE[:, :], [[P, TILES]], base=0, channel_multiplier=1, allow_small_or_imprecise_dtypes=True).then_inc(consts_ready, 1)
            pool.memset(IDENT[:, :], 0.0).then_inc(consts_ready, 1)
            pool.wait_ge(consts_ready, 4)
            pool.affine_select(out=IDENT[:, :], in_=IDENT[:, :], compare_op=ALU.not_equal, fill=1.0, base=0,
                               pattern=[[-1, P]], channel_multiplier=1).then_inc(consts_ready, 1)
            pool.wait_ge(span_in, 1)
            pool.partition_all_reduce(span[:, :, :].rearrange("p a g -> p (a g)"), span[:, :, :].rearrange("p a g -> p (a g)"),
                                      P, bass.bass_isa.ReduceOp.max).then_inc(span_red, 1)
            pool.wait_ge(range_in, 1)
            pool.partition_all_reduce(rangev[:, :], rangev[:, :], P, bass.bass_isa.ReduceOp.max).then_inc(range_red, 1)
            for k, ps in enumerate(passes):
                pool.wait_ge(ps["table_done"], 16 * BLOCKS)
                buf = gf if ps["parts"] == 1 else gh
                with pool.Fori(0, ROUNDS) as i:
                    for s in range(SLOTS):
                        pool.wait_ge(slots_free, i * SLOTS + (k * GROUPS + s + 1))
                        pool.wait_ge(idx_loaded[s], i * 16 + (k * ROUNDS * 16 + 16))
                        settle(pool)
                        for c in range(C):
                            pool.indirect_dma_start(buf[:, s, c, 0:ps["row"]], None, ps["table"][:, :],
                                                    bass.IndirectOffsetOnAxis(idx[:, s, c:c + 1], 0)).then_inc(ps["gathered"][s], 16)

        def dense_tensor(pe, k):
            ps = passes[k]
            if ps["name"] in ("dev", "sage2", "sage4"):
                return
            if ps["name"] == "gat":
                with pe.Fori(0, BLOCKS) as b:
                    pe.wait_ge(step_sem["stack_ready"], block_count("stack_ready", ps["name"], b))
                    for j in range(2 * TB):
                        last = pe.transpose(ps_turn[:, j * P:(j + 1) * P], big[:, j * P:(j + 1) * P], IDENT[:, :])
                    last.then_inc(step_sem["turned"], 1)
                    pe.wait_ge(step_sem["copied"], block_count("copied", ps["name"], b))
                    for j in range(TB):
                        for q in range(2):
                            last = pe.matmul(ps_out[:, j * D:(j + 1) * D], bigT[:, (2 * j + q) * P:(2 * j + q + 1) * P], MST[:, q, :],
                                             start=(q == 0), stop=(q == 1))
                    last.then_inc(step_sem["product"], 1)
                return
            with pe.Fori(0, BLOCKS) as b:
                pe.wait_ge(step_sem["stack_ready"], block_count("stack_ready", ps["name"], b))
                settle(pe)
                kdim = 2 * LAT if ps["name"] == "sage3" else 2 * D
                for j in range(TB):
                    last = pe.transpose(ps_turn[0:kdim, j * P:(j + 1) * P], big[:, j * kdim:(j + 1) * kdim], IDENT[:, :])
                last.then_inc(step_sem["turned"], 1)
                wa = {"gine": W1S, "sage1": S1, "sage3": S3}[ps["name"]]
                wb = {"gine": W2, "sage1": S2, "sage3": S4}[ps["name"]]
                m = {"gine": D, "sage1": 2 * LAT, "sage3": 2 * D}[ps["name"]]
                pe.wait_ge(step_sem["copied"], block_count("copied", ps["name"], b))
                for q in range(2):
                    last = pe.matmul(ps_hid[:, 512 * q:512 * q + HALF], wa[:, :], bigT[0:kdim, q * HALF:(q + 1) * HALF], start=True, stop=True)
                last.then_inc(step_sem["hidden"], 1)
                pe.wait_ge(step_sem["relued"], block_count("relued", ps["name"], b))
                for j in range(TB):
                    last = pe.matmul(ps_out[:, j * m:(j + 1) * m], hid[:, j * P:(j + 1) * P], wb[:, :], start=True, stop=True)
                last.then_inc(step_sem["product"], 1)

        @block.tensor
        def _(pe):
            regs = [pe.alloc_register("pe_lo"), pe.alloc_register("pe_hi")]
            pairs, spread = pe.alloc_register("pe_pairs"), pe.alloc_register("pe_spread")
            pe.wait_ge(loaded, N_CONST)
            pe.wait_ge(consts_ready, 5)
            I64 = IDENT[0:D, 0:D]
            pe.transpose(ps_turn[:, 0:D], W[:, 0:P], I64)
            pe.transpose(ps_turn[:, D:2 * D], W[:, P:2 * P], I64)
            pe.transpose(ps_turn[0:D, 2 * D:3 * D], We[:, :], I64)
            pe.transpose(ps_turn[:, 512:512 + HID], nat1[:, :], IDENT[:, :])
            pe.transpose(ps_turn[:, 640:640 + 2 * LAT], nat2[:, :], I64)
            pe.transpose(ps_turn[0:2 * LAT, 704:704 + HID], nat3[:, :], IDENT[:, :])
            pe.transpose(ps_turn[:, 832:832 + 2 * D], nat4[:, :], IDENT[:, :]).then_inc(prep_t, 1)
            pe.wait_ge(prep_done, 1)
            for k in range(2):
                pe.matmul(ps_turn[:, 1024 + 64 * k:1088 + 64 * k], BD[:, k, :], Wl[:, k, :], start=True, stop=True)
            pe.matmul(ps_turn[:, 1536:1536 + HID], WeT[:, :, :].rearrange("p a b -> p (a b)"), W1[:, :], start=True, stop=True)
            for k in range(2):
                last = pe.matmul(ps_hid[:, 0:D], biasb[:, k, :], Wl[:, k, :], start=(k == 0), stop=(k == 1))
            last.then_inc(prep_t, 1)

            pe.wait_ge(x_loaded, N_X)
            pe.wait_ge(x_zeroed, 1)
            pe.wait_ge(prep_done, 2)
            with pe.Fori(0, BLOCKS) as b:
                pe.wait_ge(score_in, b + 1)
                settle(pe)
                for j in range(TB):
                    last = pe.transpose(ps_turn[0:D, j * P:(j + 1) * P],
                                        big[:, j * D:(j + 1) * D], IDENT[:, :])
                last.then_inc(score_t, 1)
                pe.wait_ge(score_c, b + 1)
                for j in range(TB):
                    last = pe.matmul(ps_out[:, j * 2 * H:(j + 1) * 2 * H], bigT[0:D, j * P:(j + 1) * P], Wa[:, :], start=True, stop=True)
                last.then_inc(score_mm, 1)

            for k, ps in enumerate(passes):
                gat = ps["name"] == "gat"
                n, parts = ps["n"], ps["parts"]
                pe.reg_mov(pairs, 0)
                if gat:
                    pe.reg_mov(spread, 0)
                pe.wait_ge(pass_open, k + 1)
                with pe.Fori(0, ROUNDS) as i:
                    for s in range(SLOTS):
                        g = i * SLOTS + s
                        lo, hi = span_of(pe, regs, g)
                        if gat:
                            pe.wait_ge(logit_ready, g)
                            pe.matmul(ps_exp[:, :, :].rearrange("p c k -> p (c k)"), ZERO[:, :], ZERO[:, 0:C * 2 * H],
                                      start=True, stop=False)
                            with pe.Fori(lo, hi) as t:
                                pe.reg_add(spread, spread, 1)
                                pe.wait_ge(nodehot_ready, pe.snap(spread, min_val=1, max_val=GROUPS * TILES))
                                for c in range(C):
                                    for q in range(3):
                                        last = pe.matmul(ps_exp[:, c, :], nodehot[:, c * P:(c + 1) * P],
                                                         VALS[:, bass.ds(t, 1), q, :].rearrange("p a k -> p (a k)"),
                                                         start=False, stop=False)
                                last.then_inc(expand_done, 1)
                            pe.matmul(ps_exp[:, :, :].rearrange("p c k -> p (c k)"), ZERO[:, :], ZERO[:, 0:C * 2 * H],
                                      start=False, stop=True).then_inc(expand_open, 1)
                        else:
                            pe.wait_ge(ps["gathered"][s], i * (16 * C) + 16 * C)
                            settle(pe)
                            if ps["name"] == "gine":
                                pe.wait_ge(edges_loaded[s], i * 16 + 16)
                                settle(pe)
                        with pe.Fori(lo, hi) as t:
                            pe.reg_add(pairs, pairs, 1)
                            pe.wait_ge(ps["onehot_ready"], pe.snap(pairs, min_val=1, max_val=GROUPS * TILES))
                            for c in range(C):
                                for q in range(parts):
                                    if gat:
                                        lhs, rhs = onehot[:, c, :], msg[:, c, :]
                                    elif parts == 1:
                                        lhs, rhs = onehot[:, c, :], gf[:, s, c, 0:n]
                                    else:
                                        lhs, rhs = onehot_h[:, c, :], gh[:, s, c, q * n:(q + 1) * n]
                                    last = pe.matmul(ps_agg[:, 0:n], lhs, rhs, start=(c == 0 and q == 0),
                                                     stop=(c == C - 1 and q == parts - 1))
                            last.then_inc(ps["agg_done"], 1)
                dense_tensor(pe, k)

        @block.scalar
        def _(act):
            with act.Fori(0, BLOCKS) as b:
                act.wait_ge(score_t, b + 1)
                act.activation(bigT[0:D, 0:TB * P], ps_turn[0:D, 0:TB * P], ACT.Copy).then_inc(score_c, 1)
            act.wait_ge(self_in, 1)
            act.activation(WSELF[:, :, :], WSELF[:, :, :], ACT.Exp).then_inc(self_exp, 1)
            for k, ps in enumerate(passes):
                name = ps["name"]
                if name == "gat":
                    with act.Fori(0, GROUPS) as g:
                        act.wait_ge(logit_ready, g + 1)
                        act.activation(wts[:, :, :], lg[:, 2, :, :], ACT.Exp).then_inc(weight_ready, 1)
                with act.Fori(0, BLOCKS) as b:
                    if name == "gat":
                        act.wait_ge(step_sem["turned"], block_count("turned", ps["name"], b))
                        act.activation(bigT[:, :], ps_turn[:, 0:TB * H * D], ACT.Copy).then_inc(step_sem["copied"], 1)
                    if name in ("gine", "sage1", "sage3"):
                        kdim = 2 * LAT if name == "sage3" else 2 * D
                        bias = {"gine": b1, "sage1": sb1, "sage3": sb3}[name]
                        act.wait_ge(step_sem["turned"], block_count("turned", ps["name"], b))
                        act.activation(bigT[0:kdim, 0:TB * P], ps_turn[0:kdim, 0:TB * P], ACT.Copy).then_inc(step_sem["copied"], 1)
                        act.wait_ge(step_sem["hidden"], block_count("hidden", ps["name"], b))
                        act.activation(hid[:, :].rearrange("p (q n) -> p q n", q=2),
                                       ps_hid[:, :].rearrange("p (q n) -> p q n", q=2)[:, :, 0:HALF], ACT.Relu,
                                       bias=bias[:, :]).then_inc(step_sem["relued"], 1)
                    if name == "dev":
                        act.wait_ge(dev_in, b + 1)
                        act.activation(tmp[:, 1, 0:TB * D], tmp[:, 1, 0:TB * D], ACT.Sqrt).then_inc(dev_out, 1)
                    if name in ("gat", "dev", "gine", "sage4"):
                        act.wait_ge(step_sem["var_ready"], block_count("var_ready", ps["name"], b))
                        act.activation(small[:, 2, 0:TB], small[:, 1, 0:TB], ACT.Sqrt).then_inc(step_sem["std_ready"], 1)

        def same(dst, src):
            return nc.vector.tensor_scalar(dst, src, 1.0, None, ALU.mult)

        def dense_vector(ve, step, k, split):
            ps = passes[k]
            name, acc = ps["name"], acc_of[k]

            def blocked(ap, b):
                return ap[:, bass.ds(b * TB, TB), :]

            def view(buf, cols):
                return buf.rearrange("p (t k) -> p t k", t=TB) if cols is None else buf[:, 0:TB * cols].rearrange("p (t k) -> p t k", t=TB)

            def bcast(ap, cols):
                return ap.unsqueeze(2).broadcast_to([P, TB, cols])

            def row(ap, cols=D):
                return ap.unsqueeze(1).broadcast_to([P, TB, cols])

            def layer_norm(b, y, dst):
                mean, var, std = small[:, 0, 0:TB], small[:, 1, 0:TB], small[:, 2, 0:TB]
                sq = view(tmp[:, 3, :], D)
                step(ve.tensor_reduce(mean, y, X_AXIS, ALU.add))
                step(ve.tensor_scalar(mean, mean, 1.0 / D, None, ALU.mult))
                step(ve.tensor_tensor(y, y, bcast(mean, D), ALU.subtract))
                step(ve.tensor_tensor(sq, y, y, ALU.mult))
                step(ve.tensor_reduce(var, sq, X_AXIS, ALU.add))
                step(ve.tensor_scalar(var, var, 1.0 / D, LN_EPS, ALU.mult, ALU.add))
                ve.sem_inc(step_sem["var_ready"], 1)
                ve.wait_ge(step_sem["std_ready"], block_count("std_ready", ps["name"], b))
                step(ve.reciprocal(std, std))
                step(ve.tensor_tensor(dst, y, bcast(std, D), ALU.mult))
                return 8

            def store_parts(b, value, cols):
                nxt = passes[k + 1]
                ve.wait_ge(nxt["table_done"], b * 16)
                split(value, view(rows, 3 * cols), lambda d, q: d[:, :, q * cols:(q + 1) * cols])
                ve.sem_inc(rows_ready[k + 1], 1)

            y = view(tmp[:, 0, :], D)
            if name == "gat":
                step(ve.tensor_copy(DEG[:, :], acc[:, :, GATW - 1]))
                step(ve.tensor_scalar(RDEG[:, :], DEG[:, :], 1.0, None, ALU.max))
                step(ve.reciprocal(RDEG[:, :], RDEG[:, :]))
            if name == "dev":
                step(ve.tensor_scalar(small[:, 4, :], DEG[:, :], 1e-8, None, ALU.max))
                step(ve.reciprocal(small[:, 4, :], small[:, 4, :]))
                step(ve.tensor_scalar(small[:, 5, :], DEG[:, :], 1.0, None, ALU.is_gt))
            if name == "gine":
                step(ve.tensor_scalar(epsb[:, :], epsb[:, :], 1.0, None, ALU.add))
            per = {"gat": 23, "dev": 18, "gine": 20, "sage1": 9, "sage2": 8, "sage3": 9, "sage4": 11}[name]
            with ve.Fori(0, BLOCKS) as b:
                step.loop(b, per)
                a = blocked(acc, b)
                xb = blocked(X, b)
                if name == "gat":
                    sums = a[:, :, 0:H * D].rearrange("p t (h d) -> p t h d", h=H)
                    b4 = big[:, :].rearrange("p (t h d) -> p t h d", t=TB, h=H)
                    wself = WSELF[:, bass.ds(b * TB, TB), :]
                    dd = small[:, 6, 0:TB * H].rearrange("p (t h) -> p t h", t=TB)
                    step(ve.tensor_tensor(b4, xb.unsqueeze(2).broadcast_to([P, TB, H, D]), wself.unsqueeze(3).broadcast_to([P, TB, H, D]), ALU.mult))
                    step(ve.tensor_tensor(dd, a[:, :, H * D:H * D + H], wself, ALU.add))
                    step(ve.tensor_scalar(dd, dd, 1e-16, None, ALU.add))
                    step(ve.reciprocal(dd, dd))
                    step(ve.tensor_tensor(sums, sums, b4, ALU.add))
                    step(ve.tensor_tensor(b4, sums, dd.unsqueeze(3).broadcast_to([P, TB, H, D]), ALU.mult))
                    ve.sem_inc(step_sem["stack_ready"], 1)
                    ve.wait_ge(step_sem["product"], block_count("product", ps["name"], b))
                    step(ve.tensor_tensor(y, view(ps_out, D), xb, ALU.add))
                    step(ve.tensor_tensor(y, y, row(CV[:, :]), ALU.add))
                    layer_norm(b, y, xb)
                    both = view(big, 2 * D)
                    step(same(both[:, :, 0:D], xb))
                    step(ve.tensor_tensor(both[:, :, D:2 * D], xb, xb, ALU.mult))
                    store_parts(b, both, 2 * D)
                if name == "dev":
                    r = small[:, 4, bass.ds(b * TB, TB)]
                    many = small[:, 5, bass.ds(b * TB, TB)]
                    v = view(tmp[:, 1, :], D)
                    step(ve.tensor_tensor(y, a[:, :, 0:D], bcast(r, D), ALU.mult))
                    step(ve.tensor_tensor(y, y, y, ALU.mult))
                    step(ve.tensor_tensor(v, a[:, :, D:2 * D], bcast(r, D), ALU.mult))
                    step(ve.tensor_tensor(v, v, y, ALU.subtract))
                    step(ve.tensor_scalar(v, v, 0.0, None, ALU.max))
                    step(ve.tensor_scalar(y, v, 0.0, None, ALU.is_gt))
                    step(ve.tensor_tensor(y, y, bcast(many, D), ALU.mult))
                    step(ve.tensor_scalar(v, v, 1e-30, None, ALU.max))
                    ve.sem_inc(dev_in, 1)
                    ve.wait_ge(dev_out, b + 1)
                    step(ve.tensor_tensor(v, v, y, ALU.mult))
                    step(ve.tensor_tensor(y, v, xb, ALU.add))
                    layer_norm(b, y, xb)
                    ve.sem_inc(rows_ready[k + 1], 1)
                if name == "gine":
                    stack = view(big, 2 * D)
                    u = view(tmp[:, 2, :], D)
                    step(ve.tensor_tensor(u, row(Web[:, :]), bcast(DEG[:, bass.ds(b * TB, TB)], D), ALU.mult))
                    step(ve.tensor_tensor(u, u, a[:, :, 0:D], ALU.add))
                    step(ve.scalar_tensor_tensor(stack[:, :, 0:D], xb, epsb[:, :], u, ALU.mult, ALU.add))
                    step(same(stack[:, :, D:2 * D], a[:, :, D:2 * D]))
                    ve.sem_inc(step_sem["stack_ready"], 1)
                    ve.wait_ge(step_sem["product"], block_count("product", ps["name"], b))
                    step(ve.tensor_tensor(y, view(ps_out, D), xb, ALU.add))
                    step(ve.tensor_tensor(y, y, row(b2[:, :]), ALU.add))
                    layer_norm(b, y, xb)
                    step(same(y, xb))
                    store_parts(b, y, D)
                if name == "sage1":
                    stack = view(big, 2 * D)
                    step(ve.tensor_tensor(stack[:, :, 0:D], a, bcast(RDEG[:, bass.ds(b * TB, TB)], D), ALU.mult))
                    step(same(stack[:, :, D:2 * D], xb))
                    ve.sem_inc(step_sem["stack_ready"], 1)
                    ve.wait_ge(step_sem["product"], block_count("product", ps["name"], b))
                    prod = view(ps_out, 2 * LAT)
                    pv = view(tmp[:, 0, :], LAT)
                    step(ve.tensor_copy(pv, prod[:, :, 0:LAT]))
                    step(ve.tensor_tensor(blocked(Q2, b), prod[:, :, LAT:2 * LAT], row(sb2[:, :], LAT), ALU.add))
                    store_parts(b, pv, LAT)
                if name == "sage2":
                    zb = blocked(Z, b)
                    pv = view(tmp[:, 0, :], LAT)
                    step(ve.tensor_tensor(zb, a, bcast(RDEG[:, bass.ds(b * TB, TB)], LAT), ALU.mult))
                    step(ve.tensor_tensor(zb, zb, blocked(Q2, b), ALU.add))
                    step(same(pv, zb))
                    store_parts(b, pv, LAT)
                if name == "sage3":
                    stack = view(big, 2 * LAT)
                    step(ve.tensor_tensor(stack[:, :, 0:LAT], a, bcast(RDEG[:, bass.ds(b * TB, TB)], LAT), ALU.mult))
                    step(same(stack[:, :, LAT:2 * LAT], blocked(Z, b)))
                    ve.sem_inc(step_sem["stack_ready"], 1)
                    ve.wait_ge(step_sem["product"], block_count("product", ps["name"], b))
                    prod = view(ps_out, 2 * D)
                    step(ve.tensor_copy(y, prod[:, :, 0:D]))
                    step(ve.tensor_tensor(blocked(Q4, b), prod[:, :, D:2 * D], row(sb4[:, :]), ALU.add))
                    store_parts(b, y, D)
                if name == "sage4":
                    step(ve.tensor_tensor(y, a, bcast(RDEG[:, bass.ds(b * TB, TB)], D), ALU.mult))
                    step(ve.tensor_tensor(y, y, blocked(Q4, b), ALU.add))
                    step(ve.tensor_tensor(y, y, xb, ALU.add))
                    layer_norm(b, y, xb)
                    ve.sem_inc(rows_ready[k + 1], 1)
            step.close(BLOCKS)

        @block.vector
        def _(ve):
            step = Chain(ve, chain_sem)
            regs = [ve.alloc_register("ve_lo"), ve.alloc_register("ve_hi")]
            pairs, spread = ve.alloc_register("ve_pairs"), ve.alloc_register("ve_spread")

            step(ve.memset(X[:, TILES - 1, :], 0.0))
            ve.sem_inc(x_zeroed, 1)
            step(ve.memset(ZERO[:, :], 0.0))
            step(ve.memset(BD[:, :, :], 0.0))
            step(ve.memset(gathered[:, :], 0.0))
            step(ve.memset(msg[:, :, GATW - 1:GATW], 1.0))
            ve.wait_ge(loaded, N_CONST)
            ve.wait_ge(consts_ready, 5)
            step(ve.tensor_copy(DST[:, :], dst_i))
            dst3 = DST[:, :].rearrange("p (g c) -> p g c", c=C)
            step(ve.tensor_reduce(span[:, 0, :], dst3, X_AXIS, ALU.min))
            step(ve.tensor_scalar(span[:, 0, :], span[:, 0, :], -1.0, None, ALU.mult))
            step(ve.tensor_reduce(span[:, 1, :], dst3, X_AXIS, ALU.max))
            ve.sem_inc(span_in, 1)

            for q in range(2):
                step(ve.tensor_tensor(att[:, q, :], att[:, q, :], W[:, :], ALU.mult))
                step(ve.tensor_reduce(Wa[:, q * H:(q + 1) * H], att[:, q, :].rearrange("p (h d) -> p h d", h=H), X_AXIS, ALU.add))
            ve.wait_ge(prep_t, 1)
            for k in range(2):
                step(ve.tensor_copy(BD[0:D, k, 0:D], ps_turn[0:D, k * D:(k + 1) * D]))
                step(ve.tensor_copy(BD[D:P, k, D:P], ps_turn[D:P, k * D:(k + 1) * D]))
                step(ve.tensor_copy(biasb[:, k, :], biasc[:, k:k + 1].broadcast_to([P, P])))
            step(ve.tensor_copy(WeT[:, 0, :], IDENT[0:D, 0:D]))
            step(ve.tensor_copy(WeT[:, 1, :], ps_turn[0:D, 2 * D:3 * D]))
            step(ve.tensor_copy(S1[:, :], ps_turn[:, 512:512 + HID]))
            step(ve.tensor_copy(S2[:, :], ps_turn[:, 640:640 + 2 * LAT]))
            step(ve.tensor_copy(S3[:, :], ps_turn[0:2 * LAT, 704:704 + HID]))
            step(ve.tensor_copy(S4[:, :], ps_turn[:, 832:832 + 2 * D]))
            ve.sem_inc(prep_done, 1)
            ve.wait_ge(prep_t, 2)
            step(ve.tensor_copy(MST[:, :, :], ps_turn[:, 1024:1024 + 2 * D].rearrange("p (k d) -> p k d", k=2)))
            step(ve.tensor_copy(W1S[:, :], ps_turn[:, 1536:1536 + HID]))
            step(ve.tensor_tensor(CV[:, :], ps_hid[:, 0:D], bl[:, :], ALU.add))
            ve.sem_inc(prep_done, 1)

            ve.wait_ge(span_red, 1)
            step(ve.tensor_scalar(span[:, 0, :], span[:, 0, :], -1.0, None, ALU.mult))
            for q in range(2):
                step(ve.tensor_copy(SPAN[:, :, q], span[:, q, :]))
            step(ve.tensor_scalar(SPAN[:, :, :], SPAN[:, :, :], int(math.log2(P)), None, ALU.arith_shift_right))
            step(ve.tensor_copy(span[:, 1, :], SPAN[:, :, 1]))
            step(ve.tensor_scalar(SPAN[:, :, 1], span[:, 1, :], 1.0, None, ALU.add))

            ve.wait_ge(x_loaded, N_X)
            with ve.Fori(0, BLOCKS) as b:
                step.loop(b, 4)
                step(same(big[:, 0:TB * D].rearrange("p (t d) -> p t d", t=TB), X[:, bass.ds(b * TB, TB), :]))
                ve.sem_inc(score_in, 1)
                ve.wait_ge(score_mm, b + 1)
                ve.wait_ge(passes[0]["table_done"], b * 16)
                scores = ps_out[:, 0:TB * 2 * H].rearrange("p (t k) -> p t k", t=TB)
                table = score_rows.rearrange("p (t k) -> p t k", t=TB)
                step(same(ASRC[:, bass.ds(b * TB, TB), :], scores))
                step(same(table[:, :, 0:D], X[:, bass.ds(b * TB, TB), :]))
                step(ve.tensor_copy(table[:, :, D:GAT_ROW], scores[:, :, 0:H]))
                ve.sem_inc(score_m, 1)
            step.close(BLOCKS)

            a_src, a_dst = ASRC[:, :, 0:H], ASRC[:, :, H:2 * H]
            step(ve.tensor_reduce(rangev[:, 0:H], a_src.rearrange("p t h -> p h t"), X_AXIS, ALU.max))
            step(ve.memset(rangev[:, H:2 * H], 0.0))
            ve.sem_inc(range_in, 1)
            ve.wait_ge(range_red, 1)
            v8 = big[:, 0:TILES * 2 * H].rearrange("p (t k) -> p t k", t=TILES)
            t8 = big[:, 1024:1024 + TILES * 2 * H // 2].rearrange("p (t k) -> p t k", t=TILES)
            top = rangev[:, 0:H].unsqueeze(1).broadcast_to([P, TILES, H])
            step(ve.tensor_copy(v8[:, :, 0:H], a_dst))
            step(ve.tensor_tensor(t8, a_dst, top, ALU.add))
            step(ve.tensor_scalar(v8[:, :, H:2 * H], t8, NEG_SLOPE, None, ALU.mult))
            step(ve.tensor_tensor(t8, t8, v8[:, :, H:2 * H], ALU.max))
            step(ve.tensor_scalar(v8[:, :, H:2 * H], t8, -1.0, None, ALU.mult))
            step(ve.tensor_tensor(WSELF[:, :, :], a_src, a_dst, ALU.add))
            step(ve.tensor_scalar(t8, WSELF[:, :, :], NEG_SLOPE, None, ALU.mult))
            step(ve.tensor_tensor(WSELF[:, :, :], WSELF[:, :, :], t8, ALU.max))
            step(ve.tensor_tensor(WSELF[:, :, :], WSELF[:, :, :], v8[:, :, H:2 * H], ALU.add))
            ve.sem_inc(self_in, 1)

            def split(value, dst, part_axis):
                for q in range(3):
                    step(ve.tensor_copy(part_axis(dst, q), value))
                    if q < 2:
                        step(ve.tensor_tensor(value, value, part_axis(dst, q), ALU.subtract))

            split(v8, VALS, lambda d, q: d[:, :, q, :])
            ve.wait_ge(self_exp, 1)

            for k, ps in enumerate(passes):
                name, n = ps["name"], ps["n"]
                gat = name == "gat"
                acc = acc_of[k]
                oh = onehot if ps["parts"] == 1 else onehot_h
                step(ve.memset(ACC[:, 0:TILES * n], 0.0))
                ve.sem_inc(pass_open, 1)
                if k == 0:
                    ve.sem_inc(slots_free, SLOTS)
                ve.reg_mov(pairs, 0)
                if gat:
                    ve.reg_mov(spread, 0)
                per = SLOTS * (4 if gat else 0)
                with ve.Fori(0, ROUNDS) as i:
                    step.loop(i, per)
                    for s in range(SLOTS):
                        g = i * SLOTS + s
                        lo, hi = span_of(ve, regs, g)
                        if gat:
                            ve.wait_ge(dstb_loaded[s], i * 16 + 16)
                            settle(ve)
                            with ve.Fori(lo, hi) as t:
                                ve.wait_ge(expand_done, ve.snap(spread, min_val=0, max_val=GROUPS * TILES))
                                ve.tensor_scalar(nodehot[:, :], dstb[:, s, :], NODE[:, bass.ds(t, 1)], None, ALU.is_equal).then_inc(nodehot_ready, 1)
                                ve.reg_add(spread, spread, 1)
                            ve.wait_ge(expand_open, g + 1)
                            ve.wait_ge(ps["gathered"][s], i * (16 * C) + 16 * C)
                            step(ve.tensor_tensor(lg[:, 0, :, :], ps_exp[:, :, 0:H], gf[:, s, :, D:D + H], ALU.add))
                            step(ve.scalar_tensor_tensor(lg[:, 1, :, :], lg[:, 0, :, :], NEG_SLOPE, lg[:, 0, :, :], ALU.mult, ALU.max))
                            ve.wait_ge(weight_ready, g)
                            step(ve.tensor_tensor(lg[:, 2, :, :], lg[:, 1, :, :], ps_exp[:, :, H:2 * H], ALU.add))
                            ve.sem_inc(logit_ready, 1)
                            ve.wait_ge(weight_ready, g + 1)
                            ve.tensor_copy(msg[:, :, H * D:H * D + H], wts[:, :, :])
                            step(ve.tensor_tensor(msg[:, :, 0:H * D].rearrange("p c (h d) -> p c h d", h=H),
                                                  gf[:, s, :, 0:D].unsqueeze(2).broadcast_to([P, C, H, D]),
                                                  wts[:, :, :].unsqueeze(3).broadcast_to([P, C, H, D]), ALU.mult))
                            settle(ve)
                        with ve.Fori(lo, hi) as t:
                            ve.scalar_tensor_tensor(oh[:, :, :], DST[:, bass.ds(g * C, C)].unsqueeze(2).broadcast_to([P, C, P]),
                                                    TBASE[:, bass.ds(t, 1)], COL[:, :].unsqueeze(1).broadcast_to([P, C, P]),
                                                    ALU.subtract, ALU.is_equal).then_inc(ps["onehot_ready"], 1)
                            ve.reg_add(pairs, pairs, 1)
                            count = ve.snap(pairs, min_val=1, max_val=GROUPS * TILES)
                            ve.wait_ge(ps["agg_done"], count)
                            a = acc[:, bass.ds(t, 1), :]
                            ve.tensor_tensor(a, a, ps_agg[:, 0:n].unsqueeze(1), ALU.add).then_inc(ps["acc_done"], 1)
                            ve.wait_ge(ps["acc_done"], count)
                        ve.sem_inc(slots_free, 1)
                step.close(ROUNDS)
                dense_vector(ve, step, k, split)



WEIGHTS = ["L0_gnn_W", "L0_gnn_att_src", "L0_gnn_att_dst", "L0_gnn_bias", "L0_gnn_Wl", "L0_gnn_bl",
           "L2_gnn_We_w", "L2_gnn_We_b", "L2_gnn_eps", "L2_gnn_W1", "L2_gnn_b1", "L2_gnn_W2", "L2_gnn_b2",
           "L3_gnn_Wl1", "L3_gnn_bl1", "L3_gnn_Wr1", "L3_gnn_Wl2", "L3_gnn_bl2", "L3_gnn_Wr2",
           "L3_gnn_Wl3", "L3_gnn_bl3", "L3_gnn_Wr3", "L3_gnn_Wl4", "L3_gnn_bl4", "L3_gnn_Wr4"]


def kernel(**inputs):
    import numpy as np
    import concourse.bacc as bacc
    from concourse.bass_utils import run_bass_kernel_spmd

    nc = bacc.Bacc("TRN2", target_bir_lowering=False, num_devices=1)
    pad = GROUPS * GE - N_EDGES
    src = np.pad(np.asarray(inputs["src"]), (0, pad), constant_values=0).reshape(GROUPS, P, C)
    dst = np.pad(np.asarray(inputs["dst"]), (0, pad), constant_values=NPAD - 1).reshape(GROUPS, P, C)
    arrays = {
        "x": np.asarray(inputs["x"]),
        "edge_attr": np.asarray(inputs["edge_attr_64"]),
        "src_r": np.ascontiguousarray(src.transpose(1, 0, 2)).reshape(P, GROUPS * C),
        "dst_r": np.ascontiguousarray(dst.transpose(1, 0, 2)).reshape(P, GROUPS * C),
        "dst_b": np.ascontiguousarray(dst.transpose(0, 2, 1)).reshape(GROUPS, GE),
    }
    for name in WEIGHTS:
        arrays[name] = np.asarray(inputs[name])
    aps = {name: nc.dram_tensor(name, a.shape, mybir.dt.from_np(a.dtype), kind="ExternalInput").ap()
           for name, a in arrays.items()}
    out = nc.dram_tensor("out", (N_NODES, D), F32, kind="ExternalOutput").ap()
    build(nc, aps["x"], aps["edge_attr"], aps["src_r"], aps["dst_r"], aps["dst_b"], {n: aps[n] for n in WEIGHTS}, out)
    r = run_bass_kernel_spmd(nc, [arrays], core_ids=[0])
    return r.results[0]["out"]
```

```python
import math
from contextlib import ExitStack

import concourse.bass as bass
from concourse import mybir

F32 = mybir.dt.float32
BF16 = mybir.dt.bfloat16
I32 = mybir.dt.int32
ALU = mybir.AluOpType
ACT = mybir.ActivationFunctionType
X_AXIS = mybir.AxisListType.X

P = 128
N_NODES = 12500
N_EDGES = 200000
D = 64
H = 4
HID = 128
LAT = 32
TILES = -(-N_NODES // P)
TAIL = N_NODES - (TILES - 1) * P
NPAD = TILES * P
C = 4
GE = P * C
SLOTS = 8
ROUNDS = -(-N_EDGES // (GE * SLOTS))
GROUPS = ROUNDS * SLOTS
FULL_GROUPS = N_EDGES // GE
EDGE_TAIL_P = (N_EDGES - FULL_GROUPS * GE) // C
TB = 7
BLOCKS = TILES // TB
HALF = TB * P // 2
NEG_SLOPE = 0.2
LN_EPS = 1e-5
GATW = H * D + H + 1
GAT_ROW = D + H
SLOTS_AT = TILES * 3 * D
assert BLOCKS * TB == TILES and SLOTS % 4 == 0 and SLOTS & (SLOTS - 1) == 0 and (N_EDGES - FULL_GROUPS * GE) % C == 0


class Chain:

    def __init__(self, eng, sem):
        self.eng, self.sem, self.base, self.it, self.per, self.n = eng, sem, 0, 0, 0, 0

    def loop(self, it, per):
        if self.per == 0:
            self.base += self.n
        self.it, self.per, self.n = it, per, 0

    def __call__(self, ins):
        self.n += 1
        ins.then_inc(self.sem, 1)
        self.eng.wait_ge(self.sem, (self.base + self.n) if self.per == 0 else self.it * self.per + (self.base + self.n))

    def close(self, trips):
        assert self.n == self.per, (self.n, self.per)
        self.base += trips * self.per
        self.it, self.per, self.n = 0, 0, 0


def build(nc, x, edge_attr, src_r, dst_r, dst_b, w, out):
    ctx = ExitStack()
    with ctx:
        def sb(name, shape, dt=F32):
            return ctx.enter_context(nc.sbuf_tensor(name, shape, dt))

        def sem(name):
            return ctx.enter_context(nc.semaphore(name))

        passes = [
            dict(name="gat", parts=1, n=GATW, row=GAT_ROW),
            dict(name="dev", parts=3, n=2 * D, row=6 * D),
            dict(name="gine", parts=1, n=2 * D, row=D),
            dict(name="sage1", parts=3, n=D, row=3 * D),
            dict(name="sage2", parts=3, n=LAT, row=3 * LAT),
            dict(name="sage3", parts=3, n=LAT, row=3 * LAT),
            dict(name="sage4", parts=3, n=D, row=3 * D),
        ]
        for ps in passes:
            dt = F32 if ps["parts"] == 1 else BF16
            ps["dt"] = dt
            ps["table"] = nc.dram_tensor(f"table_{ps['name']}", (NPAD, ps["row"]), dt, kind="Internal").ap()
            ps["table_tiles"] = ps["table"].rearrange("(t p) w -> p t w", p=P)
            for key in ("first_hot", "first_agg", "first_acc", "rest_hot", "rest_agg", "rest_acc"):
                ps[key] = sem(f"{key}_{ps['name']}")
        STORING = ["gat", "gine", "sage1", "sage2", "sage3"]
        mlp, norm = ["gine", "sage1", "sage3"], ["gat", "dev", "gine", "sage4"]
        step_users = {"stack_ready": ["gat"] + mlp, "turned": ["gat"] + mlp, "copied": ["gat"] + mlp, "hidden": mlp,
                      "relued": mlp, "product": ["gat"] + mlp, "var_ready": norm, "std_ready": norm}
        step_sem = {key: sem(key) for key in step_users}

        def block_count(key, name, b):
            return b + (step_users[key].index(name) * BLOCKS + 1)

        table_done = sem("table_done")
        gathered = [sem(f"gathered_{s}") for s in range(SLOTS)]
        idx_loaded = [sem(f"idx_loaded_{s}") for s in range(SLOTS)]
        slots_free = sem("slots_free")
        rows_free, rows_cut, messages_ready = sem("rows_free"), sem("rows_cut"), sem("messages_ready")
        score_sum, score_leaky, weight_rest = sem("score_sum"), sem("score_leaky"), sem("weight_rest")
        dstb_free = sem("dstb_free")
        dstb_loaded = [sem(f"dstb_loaded_{s}") for s in range(2)]
        edges_loaded = [sem(f"edges_loaded_{s}") for s in range(SLOTS)]
        nodehot_ready, expand_done, expand_open = sem("nodehot_ready"), sem("expand_done"), sem("expand_open")
        logit_ready, weight_ready = sem("logit_ready"), sem("weight_ready")
        loaded, consts_ready, x_loaded = sem("loaded"), sem("consts_ready"), sem("x_loaded")
        prep_v, prep_t, span_in, span_red = sem("prep_v"), sem("prep_t"), sem("span_in"), sem("span_red")
        prep_done, score_t, score_c, score_m = sem("prep_done"), sem("score_t"), sem("score_c"), sem("score_m")
        range_in, range_red, self_in, self_exp = sem("range_in"), sem("range_red"), sem("self_in"), sem("self_exp")
        chain_sem = sem("vector_step")
        out_done = sem("out_done")
        waits_passed = sem("waits_passed")
        score_mm, score_in, score_rows_free, group_numbers = sem("score_mm"), sem("score_in"), sem("score_rows_free"), sem("group_numbers")
        dev_in, dev_out = sem("dev_in"), sem("dev_out")
        pass_open = sem("pass_open")
        rows_ready = [None] + [sem(f"rows_ready_{k}") for k in range(1, len(passes) + 1)]

        X = sb("X", [P, TILES, D])
        ACC = sb("ACC", [P, TILES * GATW])
        DEG = sb("DEG", [P, TILES])
        RDEG = sb("RDEG", [P, TILES])
        DST = sb("DST", [P, (GROUPS + 1) * C])
        NODE = sb("NODE", [P, TILES])
        TBASE = sb("TBASE", [P, TILES])
        COL = sb("COL", [P, P])
        IDENT = sb("IDENT", [P, P])
        ZEROS = sb("ZEROS", [P, GATW], BF16)
        ZERO = ZEROS[:, 0:P]
        SPAN = sb("SPAN", [P, GROUPS + 1, 2], I32)
        SCHED = sb("SCHED", [P, BLOCKS + 2], I32)
        idx = sb("idx", [P, SLOTS, C], I32)
        dstb = sb("dstb", [P, 2, GE], I32)
        gat_slots = sb("gat_slots", [P, SLOTS * C * GAT_ROW])
        table_rows = sb("table_rows", [P, TB * 6 * D], BF16)
        onehots = sb("onehots", [P, 2, C * P])
        onehot = [onehots[:, q, :].rearrange("p (c v) -> p c v", c=C) for q in range(2)]
        onehot_h = [onehots[:, q, :].bitcast(BF16)[:, 0:C * P].rearrange("p (c v) -> p c v", c=C) for q in range(2)]
        nodehot = sb("nodehot", [P, GE], BF16)
        msg = sb("msg", [P, 2, C, H * D])
        wparts = sb("wparts", [P, 2, C, 3, H + 1])
        lg = sb("lg", [P, 3, C, H])
        VALS = sb("VALS", [P, TILES, 3, 2 * H], BF16)
        ASRC = sb("ASRC", [P, TILES, 2 * H])
        WSELF = sb("WSELF", [P, TILES, H])
        rangev = sb("rangev", [P, 2 * H])
        big = sb("big", [P, TB * H * D])
        dst_i = big[:, 0:GROUPS * C].bitcast(I32)
        bigT = sb("bigT", [P, TB * H * D])
        for k, ps in enumerate(passes):
            wide = {"gine": 2 * D}.get(ps["name"], ps["row"])
            n_buf = SLOTS * C * wide // (1 if ps["parts"] == 1 else 2)
            slots = gat_slots[:, :] if k == 0 else ACC[:, SLOTS_AT:SLOTS_AT + n_buf]
            assert k == 0 or SLOTS_AT + n_buf <= TILES * GATW
            slots = slots if ps["parts"] == 1 else slots.bitcast(BF16)
            ps["buf"] = slots.rearrange("p (s c w) -> p s c w", s=SLOTS, c=C)
            if k + 1 < len(passes) and passes[k + 1]["parts"] == 3:
                ps["rows"] = table_rows[:, 0:TB * passes[k + 1]["row"]].rearrange("p (t w) -> p t w", t=TB)
        tmp = sb("tmp", [P, 4, TB * D])
        tmp_flat = tmp[:, :, :].rearrange("p a k -> p (a k)")
        score_rows = tmp_flat[:, 0:TB * GAT_ROW]
        extreme = tmp_flat[:, 2 * TB * D + D:2 * TB * D + D + 2 * GROUPS].rearrange("p (a g) -> p a g", a=2)
        onehot_rest_flat = tmp_flat[:, 0:C * P]
        onehot_rest = onehot_rest_flat.rearrange("p (c v) -> p c v", c=C)
        small = sb("small", [P, 8, TILES])
        used = [0]

        def early(rows, cols):
            at = used[0]
            used[0] += cols
            return ACC[0:rows, at:at + cols]

        W = early(D, H * D)
        att = early(D, 2 * H * D).rearrange("p (a k) -> p a k", a=2)
        biasc = early(P, 2)
        biasb = early(P, 2 * P).rearrange("p (a k) -> p a k", a=2)
        BD = early(P, 2 * P).rearrange("p (a k) -> p a k", a=2)
        bl = early(P, D)
        WeT = early(D, 2 * D).rearrange("p (a k) -> p a k", a=2)
        We = early(D, D)
        W1 = early(D, HID)
        nat1, nat2 = early(HID, 2 * D), early(2 * LAT, HID)
        nat3, nat4 = early(HID, 2 * LAT), early(2 * D, HID)
        Wl = early(P, 2 * D).rearrange("p (a k) -> p a k", a=2)
        Wa = sb("Wa", [D, 2 * H])
        MST = sb("MST", [P, 2, D])
        CV = sb("CV", [P, D])
        Web = sb("Web", [P, D])
        epsb = sb("epsb", [P, 1])
        W1S = sb("W1S", [P, HID])
        b1 = sb("b1", [P, 1])
        W2 = sb("W2", [P, D])
        b2 = sb("b2", [P, D])
        S1, S2 = sb("S1", [P, HID]), sb("S2", [HID, 2 * LAT])
        S3, S4 = sb("S3", [2 * LAT, HID]), sb("S4", [HID, 2 * D])
        sb1, sb2 = sb("sb1", [P, 1]), sb("sb2", [P, LAT])
        sb3, sb4 = sb("sb3", [P, 1]), sb("sb4", [P, D])
        hid = bigT[:, TB * P:2 * TB * P]

        def psum(name, cols):
            return ctx.enter_context(nc.psum_tensor(name, [P, cols], F32))

        ps_turn = psum("ps_turn", 2048)
        ps_hid = ps_turn[:, 1024:2048]
        ps_out = psum("ps_out", 1024)
        ps_agg = psum("ps_agg", 512)
        ps_sums = [ps_out[:, 0:512], ps_agg[:, :]]
        ps_exp_all = psum("ps_exp", 512)
        ps_exp = ps_exp_all[:, 0:C * 2 * H].rearrange("p (c k) -> p c k", c=C)

        def flat(lo, n, cols):
            return ACC[:, lo * TILES:lo * TILES + TILES * cols].rearrange("p (t k) -> p t k", k=cols)

        acc_of = [flat(0, 0, ps["n"]) for ps in passes]
        Q2, Z, Q4 = flat(64, 0, LAT), flat(96, 0, LAT), flat(128, 0, D)

        const_loads = [
            (W[:, :], w["L0_gnn_W"]),
            (att[:, 0, :], w["L0_gnn_att_src"].rearrange("h d -> (h d)").partition_broadcast(D)),
            (att[:, 1, :], w["L0_gnn_att_dst"].rearrange("h d -> (h d)").partition_broadcast(D)),
            (Wl[:, :, :], w["L0_gnn_Wl"].rearrange("(k p) n -> p k n", p=P)),
            (biasc[:, 0:1], w["L0_gnn_bias"][0:P].rearrange("(p a) -> p a", a=1)),
            (biasc[:, 1:2], w["L0_gnn_bias"][P:2 * P].rearrange("(p a) -> p a", a=1)),
            (bl[:, :], w["L0_gnn_bl"].partition_broadcast(P)),
            (We[:, :], w["L2_gnn_We_w"]),
            (Web[:, :], w["L2_gnn_We_b"].partition_broadcast(P)),
            (epsb[:, :], w["L2_gnn_eps"].rearrange("a b -> (a b)").partition_broadcast(P)),
            (W1[:, :], w["L2_gnn_W1"]),
            (b1[:, :], w["L2_gnn_b1"].rearrange("(p a) -> p a", a=1)),
            (W2[:, :], w["L2_gnn_W2"]),
            (b2[:, :], w["L2_gnn_b2"].partition_broadcast(P)),
            (nat1[:, 0:D], w["L3_gnn_Wl1"]), (nat1[:, D:2 * D], w["L3_gnn_Wr1"]),
            (nat2[0:LAT, :], w["L3_gnn_Wl2"]), (nat2[LAT:2 * LAT, :], w["L3_gnn_Wr2"]),
            (nat3[:, 0:LAT], w["L3_gnn_Wl3"]), (nat3[:, LAT:2 * LAT], w["L3_gnn_Wr3"]),
            (nat4[0:D, :], w["L3_gnn_Wl4"]), (nat4[D:2 * D, :], w["L3_gnn_Wr4"]),
            (sb1[:, :], w["L3_gnn_bl1"].rearrange("(p a) -> p a", a=1)),
            (sb2[:, :], w["L3_gnn_bl2"].partition_broadcast(P)),
            (sb3[:, :], w["L3_gnn_bl3"].rearrange("(p a) -> p a", a=1)),
            (sb4[:, :], w["L3_gnn_bl4"].partition_broadcast(P)),
            (dst_i, dst_r),
        ]
        N_CONST = 16 * len(const_loads)
        N_X = 16
        block = ctx.enter_context(nc.Block())

        def upper_halves(ap):
            dims = ["a", "b", "c", "d"][:len(ap.shape) - 1]
            lead = " ".join(dims[:-1] + [""]) if len(dims) > 1 else ""
            last = dims[-1]
            axes = f"p {lead}"
            return ap.bitcast(BF16).rearrange(f"{axes}({last} two) -> {axes}{last} two", two=2)[(slice(None),) * len(ap.shape) + (1,)]

        def parts_of(n):
            return big[:, 0:n], big[:, TB * 2 * D:TB * 2 * D + n], tmp_flat[:, 2 * TB * D:2 * TB * D + n]

        def settle(eng):
            eng.sem_inc(waits_passed, 1)

        def load_span(eng, regs, g):
            eng.reg_load(regs, SPAN[0:1, bass.ds(g, 1), :].rearrange("p a b -> p (a b)"))

        def load_spans(eng, spans, s, g):
            if s % 4 == 0:
                for q in range(2):
                    eng.reg_mov(spans[5][q], spans[3][q])
                eng.reg_load([reg for pair in spans[0:5] for reg in pair], SPAN[0:1, bass.ds(g, 5), :].rearrange("p a b -> p (a b)"))

        def this_span(eng, spans, s):
            return span(eng, spans[s % 4])

        def next_span(eng, spans, s):
            return span(eng, spans[s % 4 + 1])

        def last_span(eng, spans, s):
            return span(eng, spans[s % 4 - 1 if s % 4 else 5])

        def span(eng, regs):
            return (eng.snap(regs[0], min_val=0, max_val=TILES - 1), eng.snap(regs[1], min_val=1, max_val=TILES))

        def sweep(eng, one_round, finish, dense):
            with eng.Fori(0, BLOCKS) as b:
                r0 = eng.value_load(SCHED[0:1, bass.ds(b, 1)], min_val=0, max_val=ROUNDS)
                r1 = eng.value_load(SCHED[0:1, bass.ds(b + 1, 1)], min_val=0, max_val=ROUNDS)
                with eng.If(r0 < r1):
                    with eng.Fori(r0, r1) as r:
                        one_round(nc.s_assert_within(r, 0, ROUNDS - 1, skip_runtime_bounds_check_because="r < r1 <= ROUNDS"))
                last_block = eng.value_load(SCHED[0:1, BLOCKS + 1:BLOCKS + 2], min_val=0, max_val=BLOCKS)
                with eng.If(last_block.eq(b)):
                    finish()
                dense(b)

        @block.sync
        def _(sp):
            for dst, src in const_loads:
                sp.dma_start(dst, src).then_inc(loaded, 16)
            sp.dma_start(X[:, :, :], x.rearrange("(t p) d -> p t d", p=P)).then_inc(x_loaded, 16)

            def feed(k):
                ps = passes[k]

                def load_dst(s, g):
                    sp.wait_ge(dstb_free, g + 1)
                    sp.dma_start(dstb[:, s % 2, :], dst_b[bass.ds(g, 1), :].rearrange("a e -> (a e)").partition_broadcast(P)).then_inc(dstb_loaded[s % 2], 16)

                def one(i, s, edges):
                    g = i * SLOTS + s
                    sp.wait_ge(slots_free, g + (k * GROUPS + 1))
                    sp.dma_start(idx[:, s, :], src_r[:, bass.ds(g * C, C)]).then_inc(idx_loaded[s], 16)
                    if ps["name"] == "gat":
                        load_dst(s + 1, g + 1)
                    if ps["name"] == "gine":
                        if not edges:
                            sp.sem_inc(edges_loaded[s], 16)
                        else:
                            sp.dma_start(ps["buf"][0:edges, s, :, D:2 * D],
                                         edge_attr[bass.ds(g * GE, edges * C), :].rearrange("(p c) d -> p c d", c=C)).then_inc(edges_loaded[s], 16)

                if ps["name"] == "gat":
                    load_dst(0, 0)
                if ps["name"] != "gine":
                    with sp.Fori(0, ROUNDS) as i:
                        for s in range(SLOTS):
                            one(i, s, P)
                else:
                    with sp.Fori(0, ROUNDS - 1) as i:
                        for s in range(SLOTS):
                            one(i, s, P)
                    for s in range(SLOTS):
                        g = (ROUNDS - 1) * SLOTS + s
                        one(ROUNDS - 1, s, P if g < FULL_GROUPS else EDGE_TAIL_P if g == FULL_GROUPS else 0)

            with sp.Fori(0, BLOCKS) as b:
                sp.wait_ge(score_m, b + 1)
                sp.dma_start(passes[0]["table_tiles"][:, bass.ds(b * TB, TB), :],
                             score_rows.rearrange("p (t k) -> p t k", t=TB)).then_inc(table_done, 16)
                sp.wait_ge(table_done, b * 16 + 16)
                sp.sem_inc(score_rows_free, 1)
            for k in range(len(passes)):
                feed(k)

        @block.gpsimd
        def _(pool):
            pool.iota(COL[:, :], [[1, P]], base=0, channel_multiplier=0, allow_small_or_imprecise_dtypes=True).then_inc(consts_ready, 1)
            pool.iota(TBASE[:, :], [[P, TILES]], base=0, channel_multiplier=0, allow_small_or_imprecise_dtypes=True).then_inc(consts_ready, 1)
            pool.iota(NODE[:, :], [[P, TILES]], base=0, channel_multiplier=1, allow_small_or_imprecise_dtypes=True).then_inc(consts_ready, 1)
            pool.memset(IDENT[:, :], 0.0).then_inc(consts_ready, 1)
            pool.wait_ge(consts_ready, 4)
            pool.affine_select(out=IDENT[:, :], in_=IDENT[:, :], compare_op=ALU.not_equal, fill=1.0, base=0,
                               pattern=[[-1, P]], channel_multiplier=1).then_inc(consts_ready, 1)
            pool.wait_ge(span_in, 1)
            pool.iota(big[:, 0:GROUPS], [[1, GROUPS]], base=0, channel_multiplier=0, allow_small_or_imprecise_dtypes=True).then_inc(group_numbers, 1)
            pool.partition_all_reduce(extreme[:, :, :].rearrange("p a g -> p (a g)"), extreme[:, :, :].rearrange("p a g -> p (a g)"),
                                      P, bass.bass_isa.ReduceOp.max).then_inc(span_red, 1)
            pool.wait_ge(range_in, 1)
            pool.partition_all_reduce(rangev[:, :], rangev[:, :], P, bass.bass_isa.ReduceOp.max).then_inc(range_red, 1)
            for k, ps in enumerate(passes):
                pool.wait_ge(table_done, 16 * BLOCKS * (k + 1))
                buf = ps["buf"]
                with pool.Fori(0, ROUNDS) as i:
                    for s in range(SLOTS):
                        pool.wait_ge(slots_free, i * SLOTS + (k * GROUPS + s + 1))
                        pool.wait_ge(idx_loaded[s], i * 16 + (k * ROUNDS * 16 + 16))
                        settle(pool)
                        for c in range(C):
                            pool.indirect_dma_start(buf[:, s, c, 0:ps["row"]], None, ps["table"][:, :],
                                                    bass.IndirectOffsetOnAxis(idx[:, s, c:c + 1], 0)).then_inc(gathered[s], 16)

        def dense_tensor(pe, k, b):
            ps = passes[k]
            if ps["name"] in ("dev", "sage2", "sage4"):
                return
            pe.wait_ge(step_sem["stack_ready"], block_count("stack_ready", ps["name"], b))
            settle(pe)
            if ps["name"] == "gat":
                for j in range(2 * TB):
                    last = pe.transpose(ps_turn[:, j * P:(j + 1) * P], big[:, j * P:(j + 1) * P], IDENT[:, :])
                last.then_inc(step_sem["turned"], 1)
                pe.wait_ge(step_sem["copied"], block_count("copied", ps["name"], b))
                for j in range(TB):
                    for q in range(2):
                        last = pe.matmul(ps_out[:, j * D:(j + 1) * D], bigT[:, (2 * j + q) * P:(2 * j + q + 1) * P], MST[:, q, :],
                                         start=(q == 0), stop=(q == 1))
                last.then_inc(step_sem["product"], 1)
                return
            kdim = 2 * LAT if ps["name"] == "sage3" else 2 * D
            for j in range(TB):
                last = pe.transpose(ps_turn[0:kdim, j * P:(j + 1) * P], big[:, j * kdim:(j + 1) * kdim], IDENT[:, :])
            last.then_inc(step_sem["turned"], 1)
            wa = {"gine": W1S, "sage1": S1, "sage3": S3}[ps["name"]]
            wb = {"gine": W2, "sage1": S2, "sage3": S4}[ps["name"]]
            m = {"gine": D, "sage1": 2 * LAT, "sage3": 2 * D}[ps["name"]]
            pe.wait_ge(step_sem["copied"], block_count("copied", ps["name"], b))
            for q in range(2):
                last = pe.matmul(ps_hid[:, 512 * q:512 * q + HALF], wa[:, :], bigT[0:kdim, q * HALF:(q + 1) * HALF], start=True, stop=True)
            last.then_inc(step_sem["hidden"], 1)
            pe.wait_ge(step_sem["relued"], block_count("relued", ps["name"], b))
            for j in range(TB):
                last = pe.matmul(ps_out[:, j * m:(j + 1) * m], hid[:, j * P:(j + 1) * P], wb[:, :], start=True, stop=True)
            last.then_inc(step_sem["product"], 1)

        @block.tensor
        def _(pe):
            spans = [[pe.alloc_register(f"pe_lo{q}"), pe.alloc_register(f"pe_hi{q}")] for q in range(6)]
            rest, spread = pe.alloc_register("pe_rest"), pe.alloc_register("pe_spread")
            pe.wait_ge(loaded, N_CONST)
            pe.wait_ge(consts_ready, 5)
            I64 = IDENT[0:D, 0:D]
            pe.transpose(ps_turn[:, 0:D], W[:, 0:P], I64)
            pe.transpose(ps_turn[:, D:2 * D], W[:, P:2 * P], I64)
            pe.transpose(ps_turn[0:D, 2 * D:3 * D], We[:, :], I64)
            pe.transpose(ps_turn[:, 512:512 + HID], nat1[:, :], IDENT[:, :])
            pe.transpose(ps_turn[:, 640:640 + 2 * LAT], nat2[:, :], I64)
            pe.transpose(ps_turn[0:2 * LAT, 704:704 + HID], nat3[:, :], IDENT[:, :])
            pe.transpose(ps_turn[:, 832:832 + 2 * D], nat4[:, :], IDENT[:, :]).then_inc(prep_t, 1)
            pe.wait_ge(prep_done, 1)
            for k in range(2):
                pe.matmul(ps_turn[:, 1024 + 64 * k:1088 + 64 * k], BD[:, k, :], Wl[:, k, :], start=True, stop=True)
            pe.matmul(ps_turn[:, 1536:1536 + HID], WeT[:, :, :].rearrange("p a b -> p (a b)"), W1[:, :], start=True, stop=True)
            for k in range(2):
                last = pe.matmul(ps_agg[:, 0:D], biasb[:, k, :], Wl[:, k, :], start=(k == 0), stop=(k == 1))
            last.then_inc(prep_t, 1)

            pe.wait_ge(x_loaded, N_X)
            pe.wait_ge(prep_done, 2)
            with pe.Fori(0, BLOCKS) as b:
                pe.wait_ge(score_in, b + 1)
                settle(pe)
                for j in range(TB):
                    last = pe.transpose(ps_turn[0:D, j * P:(j + 1) * P],
                                        big[:, j * D:(j + 1) * D], IDENT[:, :])
                last.then_inc(score_t, 1)
                pe.wait_ge(score_c, b + 1)
                for j in range(TB):
                    last = pe.matmul(ps_out[:, j * 2 * H:(j + 1) * 2 * H], bigT[0:D, j * P:(j + 1) * P], Wa[:, :], start=True, stop=True)
                last.then_inc(score_mm, 1)

            def pass_tensor(k):
                ps = passes[k]
                gat = ps["name"] == "gat"
                n, parts, buf = ps["n"], ps["parts"], ps["buf"]

                def aggregate(hot, s, done):
                    sums = ps_sums[s % 2]
                    if gat:
                        upper = upper_halves([*(onehots[:, q, :] for q in range(2)), onehot_rest_flat][hot])
                        for c in range(C):
                            for q in range(3):
                                pe.matmul(sums[:, H * D:H * D + (H if q else H + 1)], upper[:, c * P:(c + 1) * P],
                                          upper_halves(wparts[:, s % 2, c, q, 0:H if q else H + 1]),
                                          start=(c == 0 and q == 0), stop=(c == C - 1 and q == 2))
                    for c in range(C):
                        for q in range(parts):
                            if gat:
                                lhs, rhs = (onehot_rest if hot == 2 else onehot[hot])[:, c, :], msg[:, s % 2, c, :]
                            elif parts == 1:
                                lhs, rhs = onehot[hot][:, c, :], buf[:, s, c, 0:n]
                            else:
                                lhs, rhs = onehot_h[hot][:, c, :], buf[:, s, c, q * n:(q + 1) * n]
                            last = pe.matmul(sums[:, 0:H * D if gat else n], lhs, rhs, start=(c == 0 and q == 0), stop=(c == C - 1 and q == parts - 1))
                    last.then_inc(done, 1)

                def further_tiles(prev, lo, hi):
                    with pe.If(lo + 1 < hi):
                        with pe.Fori(lo + 1, hi) as t:
                            pe.reg_add(rest, rest, 1)
                            pe.wait_ge(ps["rest_hot"], pe.snap(rest, min_val=1, max_val=GROUPS * TILES))
                            aggregate(2 if gat else prev % 2, prev, ps["rest_agg"])

                def expand(g, lo, hi):
                    pe.wait_ge(logit_ready, g + 1)
                    pe.matmul(ps_exp_all[:, 0:C * 2 * H], ZERO[:, :], ZERO[:, 0:C * 2 * H], start=True, stop=False)
                    with pe.Fori(lo, hi) as t:
                        pe.reg_add(spread, spread, 1)
                        pe.wait_ge(nodehot_ready, pe.snap(spread, min_val=1, max_val=GROUPS * TILES))
                        for c in range(C):
                            for q in range(3):
                                last = pe.matmul(ps_exp[:, c, :], nodehot[:, c * P:(c + 1) * P],
                                                 VALS[:, bass.ds(t, 1), q, :].rearrange("p a k -> p (a k)"),
                                                 start=False, stop=False)
                        last.then_inc(expand_done, 1)
                    pe.matmul(ps_exp_all[:, 0:C * 2 * H], ZERO[:, :], ZERO[:, 0:C * 2 * H],
                              start=False, stop=True).then_inc(expand_open, 1)

                def one_round(i):
                    for s in range(SLOTS):
                        g = i * SLOTS + s
                        load_spans(pe, spans, s, g)
                        if gat:
                            expand(g + 1, *next_span(pe, spans, s))
                        further_tiles((s - 1) % SLOTS, *last_span(pe, spans, s))
                        if gat:
                            pe.wait_ge(messages_ready, g * 2 + 2)
                        else:
                            pe.wait_ge(gathered[s], i * (16 * C) + (k * ROUNDS + 1) * 16 * C)
                        settle(pe)
                        if ps["name"] == "gine":
                            pe.wait_ge(edges_loaded[s], i * 16 + 16)
                            settle(pe)
                        pe.wait_ge(ps["first_hot"], g + 1)
                        settle(pe)
                        pe.wait_ge(ps["first_acc"], g + 1)
                        settle(pe)
                        aggregate(s % 2, s, ps["first_agg"])

                for reg, value in ((rest, 0), (spans[3][0], 0), (spans[3][1], 1)):
                    pe.reg_mov(reg, value)
                pe.wait_ge(pass_open, k + 1)
                if gat:
                    pe.reg_mov(spread, 0)
                    pe.sem_inc(expand_done, 1)
                    load_span(pe, spans[0], 0)
                    expand(0, *span(pe, spans[0]))
                pe.matmul(ps_agg[:, 0:n], ZERO[:, :], ZEROS[:, 0:n], start=True, stop=True).then_inc(ps["first_agg"], 1)
                sweep(pe, one_round, lambda: further_tiles(SLOTS - 1, *span(pe, spans[3])), lambda b: dense_tensor(pe, k, b))

            for k in range(len(passes)):
                pass_tensor(k)

        @block.scalar
        def _(act):
            with act.Fori(0, BLOCKS) as b:
                act.wait_ge(score_t, b + 1)
                act.activation(bigT[0:D, 0:TB * P], ps_turn[0:D, 0:TB * P], ACT.Copy).then_inc(score_c, 1)
            act.wait_ge(self_in, 1)
            act.activation(WSELF[:, :, :], WSELF[:, :, :], ACT.Exp).then_inc(self_exp, 1)

            def one_round(i):
                for s in range(SLOTS):
                    act.wait_ge(logit_ready, i * SLOTS + (s + 2))
                    act.activation(wparts[:, s % 2, :, 0, 0:H], lg[:, 2, :, :], ACT.Exp).then_inc(weight_ready, 1)

            def dense_scalar(k, b):
                ps = passes[k]
                name = ps["name"]
                if name == "gat":
                    act.wait_ge(step_sem["turned"], block_count("turned", ps["name"], b))
                    act.activation(bigT[:, :], ps_turn[:, 0:TB * H * D], ACT.Copy).then_inc(step_sem["copied"], 1)
                if name in ("gine", "sage1", "sage3"):
                    kdim = 2 * LAT if name == "sage3" else 2 * D
                    bias = {"gine": b1, "sage1": sb1, "sage3": sb3}[name]
                    act.wait_ge(step_sem["turned"], block_count("turned", ps["name"], b))
                    act.activation(bigT[0:kdim, 0:TB * P], ps_turn[0:kdim, 0:TB * P], ACT.Copy).then_inc(step_sem["copied"], 1)
                    act.wait_ge(step_sem["hidden"], block_count("hidden", ps["name"], b))
                    act.activation(hid.rearrange("p (q n) -> p q n", q=2),
                                   ps_hid.rearrange("p (q n) -> p q n", q=2)[:, :, 0:HALF], ACT.Relu,
                                   bias=bias[:, :]).then_inc(step_sem["relued"], 1)
                if name == "dev":
                    act.wait_ge(dev_in, b + 1)
                    act.activation(tmp[:, 1, 0:TB * D], tmp[:, 1, 0:TB * D], ACT.Sqrt).then_inc(dev_out, 1)
                if name in ("gat", "dev", "gine", "sage4"):
                    act.wait_ge(step_sem["var_ready"], block_count("var_ready", ps["name"], b))
                    act.activation(small[:, 2, 0:TB], small[:, 1, 0:TB], ACT.Sqrt).then_inc(step_sem["std_ready"], 1)
                act.wait_ge(rows_ready[k + 1], b + 1)
                if name == "sage4":
                    act.dma_start(out[bass.ds(b * (TB * P), TB * P), :].rearrange("(t p) d -> p t d", p=P),
                                  X[:, bass.ds(b * TB, TB), :]).then_inc(out_done, 16)
                    return
                nxt = passes[k + 1]
                source = X[:, bass.ds(b * TB, TB), :]
                if name in STORING:
                    source, cols = ps["rows"], nxt["row"] // 3
                    act.wait_ge(table_done, b * 16 + (k + 1) * BLOCKS * 16)
                    settle(act)
                    for q in range(3):
                        act.activation(source[:, :, q * cols:(q + 1) * cols],
                                       upper_halves(parts_of(TB * cols)[q]).rearrange("p (t k) -> p t k", t=TB), ACT.Copy).then_inc(rows_cut, 1)
                    act.wait_ge(rows_cut, b * 3 + (STORING.index(name) * BLOCKS * 3 + 3))
                    act.sem_inc(rows_free, 1)
                act.dma_start(nxt["table_tiles"][:, bass.ds(b * TB, TB), :], source).then_inc(table_done, 16)

            for k in range(len(passes)):
                if k == 0:
                    sweep(act, one_round, lambda: None, lambda b: dense_scalar(0, b))
                else:
                    with act.Fori(0, BLOCKS) as b:
                        dense_scalar(k, b)
            act.wait_ge(out_done, 16 * BLOCKS)

        def same(dst, src):
            return nc.vector.tensor_scalar(dst, src, 1.0, None, ALU.mult)

        def dense_vector(ve, step, k, split, b):
            ps = passes[k]
            name, acc = ps["name"], acc_of[k]

            def blocked(ap, b):
                return ap[:, bass.ds(b * TB, TB), :]

            def view(buf, cols):
                return buf.rearrange("p (t k) -> p t k", t=TB) if cols is None else buf[:, 0:TB * cols].rearrange("p (t k) -> p t k", t=TB)

            def bcast(ap, cols):
                return ap.unsqueeze(2).broadcast_to([P, TB, cols])

            def row(ap, cols=D):
                return ap.unsqueeze(1).broadcast_to([P, TB, cols])

            def layer_norm(b, y, dst):
                mean, var, std = small[:, 0, 0:TB], small[:, 1, 0:TB], small[:, 2, 0:TB]
                sq = view(tmp[:, 3, :], D)
                step(ve.tensor_reduce(mean, y, X_AXIS, ALU.add))
                step(ve.tensor_scalar(mean, mean, 1.0 / D, None, ALU.mult))
                step(ve.tensor_tensor(y, y, bcast(mean, D), ALU.subtract))
                step(ve.tensor_tensor(sq, y, y, ALU.mult))
                step(ve.tensor_reduce(var, sq, X_AXIS, ALU.add))
                step(ve.tensor_scalar(var, var, 1.0 / D, LN_EPS, ALU.mult, ALU.add))
                ve.sem_inc(step_sem["var_ready"], 1)
                ve.wait_ge(step_sem["std_ready"], block_count("std_ready", ps["name"], b))
                step(ve.reciprocal(std, std))
                step(ve.tensor_tensor(dst, y, bcast(std, D), ALU.mult))
                return 8

            def store_parts(cols):
                v = parts_of(TB * cols)
                for q in range(2):
                    step(ve.tensor_tensor(v[q + 1], v[q], upper_halves(v[q]), ALU.subtract))
                ve.sem_inc(rows_ready[k + 1], 1)

            if name in STORING:
                ve.wait_ge(rows_free, b + (STORING.index(name) * BLOCKS + 1))
            y = view(tmp[:, 0, :], D)
            a = blocked(acc, b)
            xb = blocked(X, b)
            if name == "gat":
                deg, rdeg = DEG[:, bass.ds(b * TB, TB)], RDEG[:, bass.ds(b * TB, TB)]
                step(same(deg, a[:, :, GATW - 1]))
                step(ve.tensor_scalar(small[:, 5, 0:TB], deg, 1.0, None, ALU.max))
                step(ve.reciprocal(small[:, 5, 0:TB], small[:, 5, 0:TB]))
                step(same(rdeg, small[:, 5, 0:TB]))
                sums = a[:, :, 0:H * D].rearrange("p t (h d) -> p t h d", h=H)
                b4 = big[:, :].rearrange("p (t h d) -> p t h d", t=TB, h=H)
                wself = WSELF[:, bass.ds(b * TB, TB), :]
                dd = small[:, 6, 0:TB * H].rearrange("p (t h) -> p t h", t=TB)
                step(ve.tensor_tensor(b4, xb.unsqueeze(2).broadcast_to([P, TB, H, D]), wself.unsqueeze(3).broadcast_to([P, TB, H, D]), ALU.mult))
                step(ve.tensor_tensor(dd, a[:, :, H * D:H * D + H], wself, ALU.add))
                step(ve.tensor_scalar(dd, dd, 1e-16, None, ALU.add))
                step(ve.reciprocal(dd, dd))
                step(ve.tensor_tensor(sums, sums, b4, ALU.add))
                step(ve.tensor_tensor(b4, sums, dd.unsqueeze(3).broadcast_to([P, TB, H, D]), ALU.mult))
                ve.sem_inc(step_sem["stack_ready"], 1)
                ve.wait_ge(step_sem["product"], block_count("product", ps["name"], b))
                step(ve.tensor_tensor(y, view(ps_out, D), xb, ALU.add))
                step(ve.tensor_tensor(y, y, row(CV[:, :]), ALU.add))
                layer_norm(b, y, xb)
                both = view(big, 2 * D)
                step(same(both[:, :, 0:D], xb))
                step(ve.tensor_tensor(both[:, :, D:2 * D], xb, xb, ALU.mult))
                store_parts(2 * D)
            if name == "dev":
                r = RDEG[:, bass.ds(b * TB, TB)]
                many = small[:, 5, 0:TB]
                step(ve.tensor_scalar(many, DEG[:, bass.ds(b * TB, TB)], 1.0, None, ALU.is_gt))
                v = view(tmp[:, 1, :], D)
                step(ve.tensor_tensor(y, a[:, :, 0:D], bcast(r, D), ALU.mult))
                step(ve.tensor_tensor(y, y, y, ALU.mult))
                step(ve.tensor_tensor(v, a[:, :, D:2 * D], bcast(r, D), ALU.mult))
                step(ve.tensor_tensor(v, v, y, ALU.subtract))
                step(ve.tensor_scalar(v, v, 0.0, None, ALU.max))
                step(ve.tensor_scalar(y, v, 0.0, None, ALU.is_gt))
                step(ve.tensor_tensor(y, y, bcast(many, D), ALU.mult))
                step(ve.tensor_scalar(v, v, 1e-30, None, ALU.max))
                ve.sem_inc(dev_in, 1)
                ve.wait_ge(dev_out, b + 1)
                step(ve.tensor_tensor(v, v, y, ALU.mult))
                step(ve.tensor_tensor(y, v, xb, ALU.add))
                layer_norm(b, y, xb)
                ve.sem_inc(rows_ready[k + 1], 1)
            if name == "gine":
                stack = view(big, 2 * D)
                u = view(tmp[:, 2, :], D)
                step(ve.tensor_tensor(u, row(Web[:, :]), bcast(DEG[:, bass.ds(b * TB, TB)], D), ALU.mult))
                step(ve.tensor_tensor(u, u, a[:, :, 0:D], ALU.add))
                step(ve.scalar_tensor_tensor(stack[:, :, 0:D], xb, epsb[:, :], u, ALU.mult, ALU.add))
                step(same(stack[:, :, D:2 * D], a[:, :, D:2 * D]))
                ve.sem_inc(step_sem["stack_ready"], 1)
                ve.wait_ge(step_sem["product"], block_count("product", ps["name"], b))
                step(ve.tensor_tensor(y, view(ps_out, D), xb, ALU.add))
                step(ve.tensor_tensor(y, y, row(b2[:, :]), ALU.add))
                layer_norm(b, y, xb)
                step(same(view(big, D), xb))
                store_parts(D)
            if name == "sage1":
                stack = view(big, 2 * D)
                step(ve.tensor_tensor(stack[:, :, 0:D], a, bcast(RDEG[:, bass.ds(b * TB, TB)], D), ALU.mult))
                step(same(stack[:, :, D:2 * D], xb))
                ve.sem_inc(step_sem["stack_ready"], 1)
                ve.wait_ge(step_sem["product"], block_count("product", ps["name"], b))
                prod = view(ps_out, 2 * LAT)
                pv = view(big, LAT)
                step(ve.tensor_copy(pv, prod[:, :, 0:LAT]))
                step(ve.tensor_tensor(blocked(Q2, b), prod[:, :, LAT:2 * LAT], row(sb2[:, :], LAT), ALU.add))
                store_parts(LAT)
            if name == "sage2":
                zb = blocked(Z, b)
                pv = view(big, LAT)
                step(ve.tensor_tensor(zb, a, bcast(RDEG[:, bass.ds(b * TB, TB)], LAT), ALU.mult))
                step(ve.tensor_tensor(zb, zb, blocked(Q2, b), ALU.add))
                step(same(pv, zb))
                store_parts(LAT)
            if name == "sage3":
                stack = view(big, 2 * LAT)
                step(ve.tensor_tensor(stack[:, :, 0:LAT], a, bcast(RDEG[:, bass.ds(b * TB, TB)], LAT), ALU.mult))
                step(same(stack[:, :, LAT:2 * LAT], blocked(Z, b)))
                ve.sem_inc(step_sem["stack_ready"], 1)
                ve.wait_ge(step_sem["product"], block_count("product", ps["name"], b))
                prod = view(ps_out, 2 * D)
                step(ve.tensor_copy(view(big, D), prod[:, :, 0:D]))
                step(ve.tensor_tensor(blocked(Q4, b), prod[:, :, D:2 * D], row(sb4[:, :]), ALU.add))
                store_parts(D)
            if name == "sage4":
                step(ve.tensor_tensor(y, a, bcast(RDEG[:, bass.ds(b * TB, TB)], D), ALU.mult))
                step(ve.tensor_tensor(y, y, blocked(Q4, b), ALU.add))
                step(ve.tensor_tensor(y, y, xb, ALU.add))
                layer_norm(b, y, xb)
                ve.sem_inc(rows_ready[k + 1], 1)

        @block.vector
        def _(ve):
            step = Chain(ve, chain_sem)
            spans = [[ve.alloc_register(f"ve_lo{q}"), ve.alloc_register(f"ve_hi{q}")] for q in range(6)]
            rest, spread = ve.alloc_register("ve_rest"), ve.alloc_register("ve_spread")

            step(ve.memset(ZEROS[:, :], 0.0))
            step(ve.memset(BD[:, :, :], 0.0))
            step(ve.memset(wparts[:, :, :, :, H:H + 1], 1.0))
            step(ve.memset(DST[:, 0:C], -1.0))
            ve.wait_ge(loaded, N_CONST)
            ve.wait_ge(consts_ready, 5)
            step(ve.tensor_copy(DST[:, C:], dst_i))
            dst3 = DST[:, C:].rearrange("p (g c) -> p g c", c=C)
            step(ve.tensor_reduce(extreme[:, 0, :], dst3, X_AXIS, ALU.min))
            step(ve.tensor_scalar(extreme[:, 0, :], extreme[:, 0, :], -1.0, None, ALU.mult))
            step(ve.tensor_reduce(extreme[:, 1, :], dst3, X_AXIS, ALU.max))
            ve.sem_inc(span_in, 1)

            for q in range(2):
                step(ve.tensor_tensor(att[:, q, :], att[:, q, :], W[:, :], ALU.mult))
                step(ve.tensor_reduce(Wa[:, q * H:(q + 1) * H], att[:, q, :].rearrange("p (h d) -> p h d", h=H), X_AXIS, ALU.add))
            ve.wait_ge(prep_t, 1)
            for k in range(2):
                step(ve.tensor_copy(BD[0:D, k, 0:D], ps_turn[0:D, k * D:(k + 1) * D]))
                step(ve.tensor_copy(BD[D:P, k, D:P], ps_turn[D:P, k * D:(k + 1) * D]))
                step(ve.tensor_copy(biasb[:, k, :], biasc[:, k:k + 1].broadcast_to([P, P])))
            step(ve.tensor_copy(WeT[:, 0, :], IDENT[0:D, 0:D]))
            step(ve.tensor_copy(WeT[:, 1, :], ps_turn[0:D, 2 * D:3 * D]))
            step(ve.tensor_copy(S1[:, :], ps_turn[:, 512:512 + HID]))
            step(ve.tensor_copy(S2[:, :], ps_turn[:, 640:640 + 2 * LAT]))
            step(ve.tensor_copy(S3[:, :], ps_turn[0:2 * LAT, 704:704 + HID]))
            step(ve.tensor_copy(S4[:, :], ps_turn[:, 832:832 + 2 * D]))
            ve.sem_inc(prep_done, 1)
            ve.wait_ge(prep_t, 2)
            step(ve.tensor_copy(MST[:, :, :], ps_turn[:, 1024:1024 + 2 * D].rearrange("p (k d) -> p k d", k=2)))
            step(ve.tensor_copy(W1S[:, :], ps_turn[:, 1536:1536 + HID]))
            step(ve.tensor_tensor(CV[:, :], ps_agg[:, 0:D], bl[:, :], ALU.add))
            ve.sem_inc(prep_done, 1)

            ve.wait_ge(span_red, 1)
            ve.wait_ge(group_numbers, 1)
            step(ve.tensor_scalar(extreme[:, 0, :], extreme[:, 0, :], -1.0, None, ALU.mult))
            for q in range(2):
                step(ve.tensor_copy(SPAN[:, 0:GROUPS, q], extreme[:, q, :]))
            step(ve.tensor_scalar(SPAN[:, 0:GROUPS, :], SPAN[:, 0:GROUPS, :], int(math.log2(P)), None, ALU.arith_shift_right))
            step(ve.tensor_copy(extreme[:, 1, :], SPAN[:, 0:GROUPS, 1]))
            step(ve.tensor_scalar(SPAN[:, 0:GROUPS, 1], extreme[:, 1, :], 1.0, None, ALU.add))
            step(ve.tensor_copy(extreme[:, 0, :], SPAN[:, 0:GROUPS, 0]))
            need = small[:, 0, 0:BLOCKS]
            for b in range(BLOCKS):
                step(ve.tensor_scalar(extreme[:, 1, :], extreme[:, 0, :], float((b + 1) * TB) - 0.5, None, ALU.is_lt))
                step(ve.tensor_tensor(extreme[:, 1, :], extreme[:, 1, :], big[:, 0:GROUPS], ALU.mult))
                step(ve.tensor_reduce(need[:, b:b + 1], extreme[:, 1, :], X_AXIS, ALU.max))
            sched_i = SCHED[:, 1:BLOCKS + 1]
            step(ve.tensor_scalar(need, need, float(1 + SLOTS), None, ALU.add))
            step(ve.tensor_copy(sched_i, need))
            step(ve.tensor_scalar(sched_i, sched_i, int(math.log2(SLOTS)), None, ALU.arith_shift_right))
            step(ve.tensor_copy(need, sched_i))
            step(ve.tensor_scalar(small[:, 1, 0:BLOCKS], need, ROUNDS + 0.5, None, ALU.is_lt))
            step(ve.tensor_reduce(small[:, 2, 0:1], small[:, 1, 0:BLOCKS], X_AXIS, ALU.add))
            step(ve.tensor_copy(SCHED[:, BLOCKS + 1:BLOCKS + 2], small[:, 2, 0:1]))
            step(ve.tensor_scalar(need, need, float(ROUNDS), None, ALU.min))
            step(ve.tensor_copy(sched_i, need))
            step(ve.memset(SCHED[:, 0:1], 0))
            step(ve.memset(SPAN[:, GROUPS:GROUPS + 1, 0:1], TILES - 1))
            step(ve.memset(SPAN[:, GROUPS:GROUPS + 1, 1:2], TILES))

            ve.sem_inc(score_rows_free, 1)
            ve.wait_ge(x_loaded, N_X)
            with ve.Fori(0, BLOCKS) as b:
                step.loop(b, 4)
                step(same(big[:, 0:TB * D].rearrange("p (t d) -> p t d", t=TB), X[:, bass.ds(b * TB, TB), :]))
                ve.sem_inc(score_in, 1)
                ve.wait_ge(score_mm, b + 1)
                ve.wait_ge(score_rows_free, b + 1)
                scores = ps_out[:, 0:TB * 2 * H].rearrange("p (t k) -> p t k", t=TB)
                table = score_rows.rearrange("p (t k) -> p t k", t=TB)
                step(same(ASRC[:, bass.ds(b * TB, TB), :], scores))
                step(same(table[:, :, 0:D], X[:, bass.ds(b * TB, TB), :]))
                step(ve.tensor_copy(table[:, :, D:GAT_ROW], scores[:, :, 0:H]))
                ve.sem_inc(score_m, 1)
            step.close(BLOCKS)

            a_src, a_dst = ASRC[:, :, 0:H], ASRC[:, :, H:2 * H]
            step(ve.tensor_reduce(rangev[:, 0:H], a_src.rearrange("p t h -> p h t"), X_AXIS, ALU.max))
            step(ve.memset(rangev[:, H:2 * H], 0.0))
            ve.sem_inc(range_in, 1)
            ve.wait_ge(range_red, 1)
            v8 = big[:, 0:TILES * 2 * H].rearrange("p (t k) -> p t k", t=TILES)
            t8 = big[:, 1024:1024 + TILES * 2 * H // 2].rearrange("p (t k) -> p t k", t=TILES)
            top = rangev[:, 0:H].unsqueeze(1).broadcast_to([P, TILES, H])
            step(ve.tensor_copy(v8[:, :, 0:H], a_dst))
            step(ve.tensor_tensor(t8, a_dst, top, ALU.add))
            step(ve.tensor_scalar(v8[:, :, H:2 * H], t8, NEG_SLOPE, None, ALU.mult))
            step(ve.tensor_tensor(t8, t8, v8[:, :, H:2 * H], ALU.max))
            step(ve.tensor_scalar(v8[:, :, H:2 * H], t8, -1.0, None, ALU.mult))
            step(ve.tensor_tensor(WSELF[:, :, :], a_src, a_dst, ALU.add))
            step(ve.tensor_scalar(t8, WSELF[:, :, :], NEG_SLOPE, None, ALU.mult))
            step(ve.tensor_tensor(WSELF[:, :, :], WSELF[:, :, :], t8, ALU.max))
            step(ve.tensor_tensor(WSELF[:, :, :], WSELF[:, :, :], v8[:, :, H:2 * H], ALU.add))
            ve.sem_inc(self_in, 1)

            def split(value, dst, part_axis):
                for q in range(3):
                    step(ve.tensor_copy(part_axis(dst, q), value))
                    if q < 2:
                        step(ve.tensor_tensor(value, value, part_axis(dst, q), ALU.subtract))

            split(v8, VALS, lambda d, q: d[:, :, q, :])
            ve.wait_ge(self_exp, 1)

            ve.sem_inc(slots_free, SLOTS - 1)
            ve.sem_inc(rows_free, 1)
            ve.sem_inc(dstb_free, 2)

            def pass_vector(k):
                ps = passes[k]
                name, n, buf = ps["name"], ps["n"], ps["buf"]
                gat = name == "gat"
                acc = acc_of[k]
                oh = onehot if ps["parts"] == 1 else onehot_h

                def hot(q, cols, t):
                    return ve.scalar_tensor_tensor(onehot_rest if q == 2 else oh[q], DST[:, bass.ds(cols, C)].unsqueeze(2).broadcast_to([P, C, P]),
                                                   TBASE[:, bass.ds(t, 1)], COL[:, :].unsqueeze(1).broadcast_to([P, C, P]),
                                                   ALU.subtract, ALU.is_equal)

                def add(t, q):
                    a = acc[:, bass.ds(t, 1), :]
                    return ve.tensor_tensor(a, a, ps_sums[q][:, 0:n].unsqueeze(1), ALU.add)

                def sum_last(s, g, lo, hi, frees=True):
                    prev = (s - 1) % SLOTS
                    ve.wait_ge(ps["first_acc"], g + 1)
                    settle(ve)
                    ve.wait_ge(ps["first_agg"], g + 1)
                    add(lo, prev % 2).then_inc(ps["first_acc"], 1)
                    with ve.If(lo + 1 < hi):
                        ve.wait_ge(ps["first_acc"], g + 2)
                        settle(ve)
                        with ve.Fori(lo + 1, hi) as t:
                            hot(2 if gat else prev % 2, g * C, t).then_inc(ps["rest_hot"], 1)
                            ve.reg_add(rest, rest, 1)
                            count = ve.snap(rest, min_val=1, max_val=GROUPS * TILES)
                            ve.wait_ge(ps["rest_agg"], count)
                            add(t, prev % 2).then_inc(ps["rest_acc"], 1)
                            ve.wait_ge(ps["rest_acc"], count)
                            settle(ve)
                    if frees:
                        ve.sem_inc(slots_free, 1)

                def spread_dst(i, s, lo, hi):
                    ve.wait_ge(dstb_loaded[s % 2], i * (SLOTS // 2 * 16) + (16 * (s // 2) + 16))
                    settle(ve)
                    with ve.Fori(lo, hi) as t:
                        ve.wait_ge(expand_done, ve.snap(spread, min_val=1, max_val=GROUPS * TILES + 1))
                        ve.tensor_scalar(nodehot[:, :], dstb[:, s % 2, :], NODE[:, bass.ds(t, 1)], None, ALU.is_equal).then_inc(nodehot_ready, 1)
                        ve.reg_add(spread, spread, 1)

                def one_round(i):
                    for s in range(SLOTS):
                        g = i * SLOTS + s
                        load_spans(ve, spans, s, g)
                        lo, _ = this_span(ve, spans, s)
                        if not gat:
                            hot(s % 2, g * C + C, lo).then_inc(ps["first_hot"], 1)
                            sum_last(s, g, *last_span(ve, spans, s))
                            continue
                        weights = [wparts[:, s % 2, :, q, 0:H] for q in range(3)]
                        ve.wait_ge(expand_open, g + 1)
                        ve.sem_inc(dstb_free, 1)
                        ve.wait_ge(gathered[s], i * (16 * C) + (k * ROUNDS + 1) * 16 * C)
                        ve.tensor_tensor(lg[:, 0, :, :], ps_exp[:, :, 0:H], buf[:, s, :, D:D + H], ALU.add).then_inc(score_sum, 1)
                        hot(s % 2, g * C + C, lo).then_inc(ps["first_hot"], 1)
                        ve.wait_ge(score_sum, g + 1)
                        ve.scalar_tensor_tensor(lg[:, 1, :, :], lg[:, 0, :, :], NEG_SLOPE, lg[:, 0, :, :], ALU.mult, ALU.max).then_inc(score_leaky, 1)
                        ve.wait_ge(score_leaky, g + 1)
                        ve.tensor_tensor(lg[:, 2, :, :], lg[:, 1, :, :], ps_exp[:, :, H:2 * H], ALU.add).then_inc(logit_ready, 1)
                        spread_dst(i, s + 1, *next_span(ve, spans, s))
                        ve.wait_ge(weight_ready, g + 1)
                        ve.tensor_tensor(weights[1], weights[0], upper_halves(weights[0]), ALU.subtract).then_inc(weight_rest, 1)
                        ve.tensor_tensor(msg[:, s % 2, :, :].rearrange("p c (h d) -> p c h d", h=H),
                                         buf[:, s, :, 0:D].unsqueeze(2).broadcast_to([P, C, H, D]),
                                         weights[0].unsqueeze(3).broadcast_to([P, C, H, D]), ALU.mult).then_inc(messages_ready, 1)
                        ve.wait_ge(weight_rest, g + 1)
                        ve.tensor_tensor(weights[2], weights[1], upper_halves(weights[1]), ALU.subtract).then_inc(messages_ready, 1)
                        sum_last(s, g, *last_span(ve, spans, s))
                    ve.wait_ge(ps["first_acc"], i * SLOTS + (SLOTS + 1))
                    settle(ve)

                def finish():
                    sum_last(0, GROUPS, *span(ve, spans[3]), frees=False)
                    ve.wait_ge(ps["first_acc"], GROUPS + 2)
                    settle(ve)

                step(ve.memset(ACC[:, 0:TILES * n], 0.0))
                for reg, value in ((rest, 0), (spans[3][0], 0), (spans[3][1], 1)):
                    ve.reg_mov(reg, value)
                if gat:
                    ve.reg_mov(spread, 1)
                    ve.wait_ge(score_rows_free, BLOCKS + 1)
                    settle(ve)
                    ve.sem_inc(logit_ready, 1)
                if name == "gine":
                    step(ve.tensor_scalar(epsb[:, :], epsb[:, :], 1.0, None, ALU.add))
                ve.sem_inc(ps["first_acc"], 1)
                ve.sem_inc(pass_open, 1)
                if gat:
                    load_span(ve, spans[0], 0)
                    spread_dst(0, 0, *span(ve, spans[0]))
                per = {"gat": 24, "dev": 19, "gine": 17, "sage1": 6, "sage2": 5, "sage3": 6, "sage4": 11}[name]

                def dense(b):
                    step.loop(b, per)
                    dense_vector(ve, step, k, split, b)

                sweep(ve, one_round, finish, dense)
                step.close(BLOCKS)

            for k in range(len(passes)):
                pass_vector(k)


WEIGHTS = ["L0_gnn_W", "L0_gnn_att_src", "L0_gnn_att_dst", "L0_gnn_bias", "L0_gnn_Wl", "L0_gnn_bl",
           "L2_gnn_We_w", "L2_gnn_We_b", "L2_gnn_eps", "L2_gnn_W1", "L2_gnn_b1", "L2_gnn_W2", "L2_gnn_b2",
           "L3_gnn_Wl1", "L3_gnn_bl1", "L3_gnn_Wr1", "L3_gnn_Wl2", "L3_gnn_bl2", "L3_gnn_Wr2",
           "L3_gnn_Wl3", "L3_gnn_bl3", "L3_gnn_Wr3", "L3_gnn_Wl4", "L3_gnn_bl4", "L3_gnn_Wr4"]


def kernel(**inputs):
    import numpy as np
    import concourse.bacc as bacc
    from concourse.bass_utils import run_bass_kernel_spmd

    nc = bacc.Bacc("TRN2", target_bir_lowering=False, num_devices=1)
    pad = GROUPS * GE - N_EDGES
    src = np.pad(np.asarray(inputs["src"]), (0, pad), constant_values=0).reshape(GROUPS, P, C)
    dst = np.pad(np.asarray(inputs["dst"]), (0, pad + GE), constant_values=NPAD - 1).reshape(GROUPS + 1, P, C)
    arrays = {
        "x": np.pad(np.asarray(inputs["x"]), ((0, NPAD - N_NODES), (0, 0))),
        "edge_attr": np.asarray(inputs["edge_attr_64"]),
        "src_r": np.ascontiguousarray(src.transpose(1, 0, 2)).reshape(P, GROUPS * C),
        "dst_r": np.ascontiguousarray(dst[:GROUPS].transpose(1, 0, 2)).reshape(P, GROUPS * C),
        "dst_b": np.ascontiguousarray(dst.transpose(0, 2, 1)).reshape(GROUPS + 1, GE),
    }
    for name in WEIGHTS:
        arrays[name] = np.asarray(inputs[name])
    aps = {name: nc.dram_tensor(name, a.shape, mybir.dt.from_np(a.dtype), kind="ExternalInput").ap()
           for name, a in arrays.items()}
    out = nc.dram_tensor("out", (NPAD, D), F32, kind="ExternalOutput").ap()
    build(nc, aps["x"], aps["edge_attr"], aps["src_r"], aps["dst_r"], aps["dst_b"], {n: aps[n] for n in WEIGHTS}, out)
    r = run_bass_kernel_spmd(nc, [arrays], core_ids=[0])
    return r.results[0]["out"][:N_NODES]
```

```python
import math
from contextlib import ExitStack

import concourse.bass as bass
from concourse import mybir

F32 = mybir.dt.float32
BF16 = mybir.dt.bfloat16
I32 = mybir.dt.int32
ALU = mybir.AluOpType
ACT = mybir.ActivationFunctionType
X_AXIS = mybir.AxisListType.X

P = 128
N_NODES = 12500
N_EDGES = 200000
D = 64
H = 4
HID = 128
LAT = 32
TILES = -(-N_NODES // P)
TAIL = N_NODES - (TILES - 1) * P
NPAD = TILES * P
C = 4
GE = P * C
SLOTS = 8
ROUNDS = -(-N_EDGES // (GE * SLOTS))
GROUPS = ROUNDS * SLOTS
FULL_GROUPS = N_EDGES // GE
EDGE_TAIL_P = (N_EDGES - FULL_GROUPS * GE) // C
TB = 7
BLOCKS = TILES // TB
HALF = TB * P // 2
NEG_SLOPE = 0.2
SCORE_RANGE = 16.0
FAR = -3e38
LN_EPS = 1e-5
GATW = H * D + H + 1
GAT_ROW = D + H
SLOTS_AT = TILES * 3 * D
PAIRS = BLOCKS // 2
assert PAIRS * 2 * TB == TILES and SLOTS % 4 == 0 and SLOTS & (SLOTS - 1) == 0 and (N_EDGES - FULL_GROUPS * GE) % C == 0


class Chain:

    def __init__(self, eng, sem):
        self.eng, self.sem, self.base, self.it, self.per, self.n = eng, sem, 0, 0, 0, 0

    def loop(self, it, per):
        if self.per == 0:
            self.base += self.n
        self.it, self.per, self.n = it, per, 0

    def __call__(self, ins):
        self.n += 1
        ins.then_inc(self.sem, 1)
        self.eng.wait_ge(self.sem, (self.base + self.n) if self.per == 0 else self.it * self.per + (self.base + self.n))

    def start(self, it, per):
        self.base, self.it, self.per, self.n = per, it, per, 0

    def close(self, trips):
        assert self.n == self.per, (self.n, self.per)
        self.base += trips * self.per
        self.it, self.per, self.n = 0, 0, 0


def build(nc, x, edge_attr, src_r, dst_r, dst_b, w, out):
    ctx = ExitStack()
    with ctx:
        def sb(name, shape, dt=F32):
            return ctx.enter_context(nc.sbuf_tensor(name, shape, dt))

        def sem(name):
            return ctx.enter_context(nc.semaphore(name))

        passes = [
            dict(name="gat", parts=1, n=GATW, row=GAT_ROW),
            dict(name="dev", parts=3, n=2 * D, row=6 * D),
            dict(name="gine", parts=1, n=2 * D, row=D),
            dict(name="sage1", parts=3, n=D, row=3 * D),
            dict(name="sage2", parts=3, n=LAT, row=3 * LAT),
            dict(name="sage3", parts=3, n=LAT, row=3 * LAT),
            dict(name="sage4", parts=3, n=D, row=3 * D),
        ]
        for ps in passes:
            dt = F32 if ps["parts"] == 1 else BF16
            ps["table"] = nc.dram_tensor(f"table_{ps['name']}", (NPAD, ps["row"]), dt, kind="Internal").ap()
            ps["table_tiles"] = ps["table"].rearrange("(t p) w -> p t w", p=P)
            for key in ("first_hot", "first_agg", "first_acc", "rest_hot", "rest_agg", "rest_acc"):
                ps[key] = sem(f"{key}_{ps['name']}")
        STORING = ["gat", "gine", "sage1", "sage2", "sage3"]
        mlp, norm = ["gine", "sage1", "sage3"], ["gat", "dev", "gine", "sage4"]
        step_users = {"stack_ready": ["gat"] + mlp, "turned": ["gat"] + mlp, "copied": ["gat"] + mlp, "hidden": mlp,
                      "relued": mlp, "product": ["gat"] + mlp, "var_ready": norm, "std_ready": norm}
        step_sem = {key: sem(key) for key in step_users}

        def block_count(key, name, b):
            return b + (step_users[key].index(name) * BLOCKS + 1)

        table_done = sem("table_done")
        gathered = [sem(f"gathered_{s}") for s in range(SLOTS)]
        idx_loaded = [sem(f"idx_loaded_{s}") for s in range(SLOTS)]
        slots_free = sem("slots_free")
        rows_free, rows_cut, messages_ready = sem("rows_free"), sem("rows_cut"), sem("messages_ready")
        hot_in, hot_distance = sem("hot_in"), sem("hot_distance")
        score_sum, score_leaky, weight_rest = sem("score_sum"), sem("score_leaky"), sem("weight_rest")
        dstb_free = sem("dstb_free")
        dstb_loaded = [sem(f"dstb_loaded_{s}") for s in range(2)]
        edges_loaded = [sem(f"edges_loaded_{s}") for s in range(SLOTS)]
        nodehot_ready, expand_done, expand_open = sem("nodehot_ready"), sem("expand_done"), sem("expand_open")
        logit_ready, weight_ready = sem("logit_ready"), sem("weight_ready")
        dst_loaded, loaded, consts_ready, x_loaded = sem("dst_loaded"), sem("loaded"), sem("consts_ready"), sem("x_loaded")
        prep_t, span_in, span_red = sem("prep_t"), sem("span_in"), sem("span_red")
        prep_done, score_t, score_c, score_m = sem("prep_done"), sem("score_t"), sem("score_c"), sem("score_m")
        range_in, range_red, self_in, self_exp = sem("range_in"), sem("range_red"), sem("self_in"), sem("self_exp")
        chain_sem, late_chain_sem = sem("vector_step"), sem("vector_late_step")
        branch_ready, max_free, max_loaded, max_gathered = sem("branch_ready"), sem("max_free"), sem("max_loaded"), sem("max_gathered")
        max_diag, max_spread = sem("max_diag"), sem("max_spread")
        max_step = [sem(f"max_step_{q}") for q in range(4)]
        out_done = sem("out_done")
        waits_passed = sem("waits_passed")
        score_mm, score_in, score_rows_free, group_numbers = sem("score_mm"), sem("score_in"), sem("score_rows_free"), sem("group_numbers")
        product_read = sem("product_read")
        dev_in, dev_out = sem("dev_in"), sem("dev_out")
        pass_open = sem("pass_open")
        rows_ready = [None] + [sem(f"rows_ready_{k}") for k in range(1, len(passes) + 1)]

        X = sb("X", [P, TILES, D])
        ACC = sb("ACC", [P, TILES * GATW])
        DEG = sb("DEG", [P, TILES])
        RDEG = sb("RDEG", [P, TILES])
        DST = sb("DST", [P, (GROUPS + 1) * C])
        NODE = sb("NODE", [P, TILES])
        TBASE = sb("TBASE", [P, TILES])
        COL = sb("COL", [P, P])
        BEHIND = sb("BEHIND", [P, 1])
        IDENT = sb("IDENT", [P, P])
        ZEROS = sb("ZEROS", [P, GATW], BF16)
        ZERO = ZEROS[:, 0:P]
        SPAN = sb("SPAN", [P, GROUPS + 1, 2], I32)
        SCHED = sb("SCHED", [P, BLOCKS + 2], I32)
        idx = sb("idx", [P, SLOTS, C], I32)
        dstb = sb("dstb", [P, 2, GE], I32)
        gat_slots = sb("gat_slots", [P, SLOTS * C * GAT_ROW])
        table_rows = sb("table_rows", [P, TB * 6 * D], BF16)
        onehots = sb("onehots", [P, 2, C * P])
        onehot = [onehots[:, q, :].rearrange("p (c v) -> p c v", c=C) for q in range(2)]
        onehot_h = [onehots[:, q, :].bitcast(BF16)[:, 0:C * P].rearrange("p (c v) -> p c v", c=C) for q in range(2)]
        ONE = sb("ONE", [P, 1])
        dst_in = sb("dst_in", [P, 2, C])
        nodehot = sb("nodehot", [P, GE], BF16)
        msg = sb("msg", [P, 2, C, H * D])
        wparts = sb("wparts", [P, 2, C, 3, H + 1])
        lg = sb("lg", [P, 3, C, H])
        VALS = sb("VALS", [P, TILES, 3, 2 * H], BF16)
        ASRC = sb("ASRC", [P, TILES, 2 * H])
        WSELF = sb("WSELF", [P, TILES, H])
        rangev = sb("rangev", [P, 2 * H])
        WIDE = sb("WIDE", [P, 1], I32)
        big = sb("big", [P, TB * H * D])
        dst_i = big[:, 0:GROUPS * C].bitcast(I32)
        bigT = sb("bigT", [P, TB * H * D])
        for k, ps in enumerate(passes):
            wide = {"gine": 2 * D}.get(ps["name"], ps["row"])
            n_buf = SLOTS * C * wide // (1 if ps["parts"] == 1 else 2)
            slots = gat_slots[:, :] if k == 0 else ACC[:, SLOTS_AT:SLOTS_AT + n_buf]
            assert k == 0 or SLOTS_AT + n_buf <= TILES * GATW
            slots = slots if ps["parts"] == 1 else slots.bitcast(BF16)
            ps["buf"] = slots.rearrange("p (s c w) -> p s c w", s=SLOTS, c=C)
            if k + 1 < len(passes) and passes[k + 1]["parts"] == 3:
                ps["rows"] = table_rows[:, 0:TB * passes[k + 1]["row"]].rearrange("p (t w) -> p t w", t=TB)
        tmp = sb("tmp", [P, 4, TB * D])
        tmp_flat = tmp[:, :, :].rearrange("p a k -> p (a k)")
        score_rows = tmp_flat[:, 0:2 * TB * GAT_ROW]
        extreme = tmp_flat[:, 2 * TB * D + D:2 * TB * D + D + 2 * GROUPS].rearrange("p (a g) -> p a g", a=2)
        onehot_rest_flat = tmp_flat[:, 0:C * P]
        onehot_rest = onehot_rest_flat.rearrange("p (c v) -> p c v", c=C)
        distance = tmp_flat[:, C * P:C * P + C * P // 2].bitcast(BF16)
        onehot_rest_h = onehot_rest_flat.bitcast(BF16)[:, 0:C * P].rearrange("p (c v) -> p c v", c=C)
        small = sb("small", [P, 8, TILES])
        used = [0]

        def early(rows, cols):
            at = used[0]
            used[0] += cols
            return ACC[0:rows, at:at + cols]

        TOP = early(P, TILES * H).rearrange("p (t h) -> p t h", t=TILES)
        max_diags = early(P, H * GE).rearrange("p (h c v) -> p h c v", h=H, c=C)
        max_vals = early(P, H * GE).rearrange("p (h e) -> p h e", h=H)
        max_mask, max_ones, max_new = early(P, GE), early(P, P), early(P, H)
        W = early(D, H * D)
        att = early(D, 2 * H * D).rearrange("p (a k) -> p a k", a=2)
        biasc = early(P, 2)
        biasb = early(P, 2 * P).rearrange("p (a k) -> p a k", a=2)
        BD = early(P, 2 * P).rearrange("p (a k) -> p a k", a=2)
        bl = early(P, D)
        WeT = early(D, 2 * D).rearrange("p (a k) -> p a k", a=2)
        We = early(D, D)
        W1 = early(D, HID)
        nat1, nat2 = early(HID, 2 * D), early(2 * LAT, HID)
        nat3, nat4 = early(HID, 2 * LAT), early(2 * D, HID)
        Wl = early(P, 2 * D).rearrange("p (a k) -> p a k", a=2)
        Wa = sb("Wa", [D, 2 * H])
        MST = sb("MST", [P, 2, D])
        CV = sb("CV", [P, D])
        Web = sb("Web", [P, D])
        epsb = sb("epsb", [P, 1])
        W1S = sb("W1S", [P, HID])
        b1 = sb("b1", [P, 1])
        W2 = sb("W2", [P, D])
        b2 = sb("b2", [P, D])
        S1, S2 = sb("S1", [P, HID]), sb("S2", [HID, 2 * LAT])
        S3, S4 = sb("S3", [2 * LAT, HID]), sb("S4", [HID, 2 * D])
        sb1, sb2 = sb("sb1", [P, 1]), sb("sb2", [P, LAT])
        sb3, sb4 = sb("sb3", [P, 1]), sb("sb4", [P, D])
        hid = bigT[:, TB * P:2 * TB * P]

        def psum(name, cols):
            return ctx.enter_context(nc.psum_tensor(name, [P, cols], F32))

        ps_turn = psum("ps_turn", 2048)
        ps_hid = ps_turn[:, 1024:2048]
        ps_out = psum("ps_out", 1024)
        ps_agg = psum("ps_agg", 512)
        ps_sums = [ps_out[:, 0:512], ps_agg[:, :], ps_out[:, 512:1024]]
        ps_exp_all = psum("ps_exp", 512)
        ps_gat = ps_exp_all[:, 64:64 + TB * D]
        ps_exp = ps_exp_all[:, 0:C * 2 * H].rearrange("p (c k) -> p c k", c=C)

        def flat(lo, n, cols):
            return ACC[:, lo * TILES:lo * TILES + TILES * cols].rearrange("p (t k) -> p t k", k=cols)

        acc_of = [flat(0, 0, ps["n"]) for ps in passes]
        Q2, Z, Q4 = flat(64, 0, LAT), flat(96, 0, LAT), flat(128, 0, D)

        const_loads = [
            (W[:, :], w["L0_gnn_W"]),
            (att[:, 0, :], w["L0_gnn_att_src"].rearrange("h d -> (h d)").partition_broadcast(D)),
            (att[:, 1, :], w["L0_gnn_att_dst"].rearrange("h d -> (h d)").partition_broadcast(D)),
            (Wl[:, :, :], w["L0_gnn_Wl"].rearrange("(k p) n -> p k n", p=P)),
            (biasc[:, 0:1], w["L0_gnn_bias"][0:P].rearrange("(p a) -> p a", a=1)),
            (biasc[:, 1:2], w["L0_gnn_bias"][P:2 * P].rearrange("(p a) -> p a", a=1)),
            (bl[:, :], w["L0_gnn_bl"].partition_broadcast(P)),
            (We[:, :], w["L2_gnn_We_w"]),
            (Web[:, :], w["L2_gnn_We_b"].partition_broadcast(P)),
            (epsb[:, :], w["L2_gnn_eps"].rearrange("a b -> (a b)").partition_broadcast(P)),
            (W1[:, :], w["L2_gnn_W1"]),
            (b1[:, :], w["L2_gnn_b1"].rearrange("(p a) -> p a", a=1)),
            (W2[:, :], w["L2_gnn_W2"]),
            (b2[:, :], w["L2_gnn_b2"].partition_broadcast(P)),
            (nat1[:, 0:D], w["L3_gnn_Wl1"]), (nat1[:, D:2 * D], w["L3_gnn_Wr1"]),
            (nat2[0:LAT, :], w["L3_gnn_Wl2"]), (nat2[LAT:2 * LAT, :], w["L3_gnn_Wr2"]),
            (nat3[:, 0:LAT], w["L3_gnn_Wl3"]), (nat3[:, LAT:2 * LAT], w["L3_gnn_Wr3"]),
            (nat4[0:D, :], w["L3_gnn_Wl4"]), (nat4[D:2 * D, :], w["L3_gnn_Wr4"]),
            (sb1[:, :], w["L3_gnn_bl1"].rearrange("(p a) -> p a", a=1)),
            (sb2[:, :], w["L3_gnn_bl2"].partition_broadcast(P)),
            (sb3[:, :], w["L3_gnn_bl3"].rearrange("(p a) -> p a", a=1)),
            (sb4[:, :], w["L3_gnn_bl4"].partition_broadcast(P)),
        ]
        N_CONST = 16 * len(const_loads)
        block = ctx.enter_context(nc.Block())

        def upper_halves(ap):
            dims = ["a", "b", "c", "d"][:len(ap.shape) - 1]
            lead = " ".join(dims[:-1] + [""]) if len(dims) > 1 else ""
            last = dims[-1]
            axes = f"p {lead}"
            return ap.bitcast(BF16).rearrange(f"{axes}({last} two) -> {axes}{last} two", two=2)[(slice(None),) * len(ap.shape) + (1,)]

        def parts_of(n):
            return big[:, 0:n], big[:, TB * 2 * D:TB * 2 * D + n], tmp_flat[:, 2 * TB * D:2 * TB * D + n]

        def wide(eng):
            return eng.value_load(WIDE[0:1, 0:1], min_val=0, max_val=1)

        def settle(eng):
            eng.sem_inc(waits_passed, 1)

        def load_span(eng, regs, g):
            eng.reg_load(regs, SPAN[0:1, bass.ds(g, 1), :].rearrange("p a b -> p (a b)"))

        def load_spans(eng, spans, s, g):
            if s % 4 == 0:
                for q in range(2):
                    eng.reg_mov(spans[5][q], spans[3][q])
                eng.reg_load([reg for pair in spans[0:5] for reg in pair], SPAN[0:1, bass.ds(g, 5), :].rearrange("p a b -> p (a b)"))

        def this_span(eng, spans, s):
            return span(eng, spans[s % 4])

        def next_span(eng, spans, s):
            return span(eng, spans[s % 4 + 1])

        def last_span(eng, spans, s):
            return span(eng, spans[s % 4 - 1 if s % 4 else 5])

        def span(eng, regs):
            return (eng.snap(regs[0], min_val=0, max_val=TILES - 1), eng.snap(regs[1], min_val=1, max_val=TILES))

        def sweep(eng, one_round, finish, dense, late=None):
            with eng.Fori(0, BLOCKS) as b:
                r0 = eng.value_load(SCHED[0:1, bass.ds(b, 1)], min_val=0, max_val=ROUNDS)
                r1 = eng.value_load(SCHED[0:1, bass.ds(b + 1, 1)], min_val=0, max_val=ROUNDS)
                with eng.If(r0 < r1):
                    with eng.Fori(r0, r1) as r:
                        one_round(nc.s_assert_within(r, 0, ROUNDS - 1, skip_runtime_bounds_check_because="r < r1 <= ROUNDS"))
                last_block = eng.value_load(SCHED[0:1, BLOCKS + 1:BLOCKS + 2], min_val=0, max_val=BLOCKS)
                with eng.If(last_block.eq(b)):
                    finish()
                if late is None:
                    dense(b)
                else:
                    dense(b, lambda: late_half(eng, b, late))
            if late is not None:
                late(BLOCKS - 1)

        def late_half(eng, b, late):
            with eng.If(b > 0):
                late(nc.s_assert_within(b - 1, 0, BLOCKS - 1, skip_runtime_bounds_check_because="b > 0"))

        @block.sync
        def _(sp):
            for dst, src in const_loads:
                sp.dma_start(dst, src).then_inc(loaded, 16)

            def feed(k):
                ps = passes[k]

                def load_dst(s, g):
                    sp.wait_ge(dstb_free, g + 1)
                    sp.dma_start(dstb[:, s % 2, :], dst_b[bass.ds(g, 1), :].rearrange("a e -> (a e)").partition_broadcast(P)).then_inc(dstb_loaded[s % 2], 16)

                def one(i, s, edges):
                    g = i * SLOTS + s
                    sp.wait_ge(slots_free, g + (k * GROUPS + 1))
                    sp.dma_start(idx[:, s, :], src_r[:, bass.ds(g * C, C)]).then_inc(idx_loaded[s], 16)
                    if ps["name"] == "gat":
                        load_dst(s + 1, g + 1)
                    if ps["name"] == "gine":
                        if not edges:
                            sp.sem_inc(edges_loaded[s], 16)
                        else:
                            sp.dma_start(ps["buf"][0:edges, s, :, D:2 * D],
                                         edge_attr[bass.ds(g * GE, edges * C), :].rearrange("(p c) d -> p c d", c=C)).then_inc(edges_loaded[s], 16)

                if ps["name"] == "gat":
                    load_dst(0, 0)
                if ps["name"] != "gine":
                    with sp.Fori(0, ROUNDS) as i:
                        for s in range(SLOTS):
                            one(i, s, P)
                else:
                    with sp.Fori(0, ROUNDS - 1) as i:
                        for s in range(SLOTS):
                            one(i, s, P)
                    for s in range(SLOTS):
                        g = (ROUNDS - 1) * SLOTS + s
                        one(ROUNDS - 1, s, P if g < FULL_GROUPS else EDGE_TAIL_P if g == FULL_GROUPS else 0)

            with sp.Fori(0, PAIRS) as b:
                sp.wait_ge(score_m, b + 1)
                sp.dma_start(passes[0]["table_tiles"][:, bass.ds(b * (2 * TB), 2 * TB), :],
                             score_rows.rearrange("p (t k) -> p t k", t=2 * TB)).then_inc(table_done, 16)
                sp.wait_ge(table_done, b * 16 + 16)
                sp.sem_inc(score_rows_free, 1)
            sp.wait_ge(branch_ready, 1)
            with sp.If(wide(sp) > 0):
                with sp.Fori(0, GROUPS) as g:
                    sp.wait_ge(max_free, g + 1)
                    sp.dma_start(idx[:, 0, :], src_r[:, bass.ds(g * C, C)]).then_inc(max_loaded, 16)
                    sp.dma_start(dstb[:, 0, :], dst_b[bass.ds(g, 1), :].rearrange("a e -> (a e)").partition_broadcast(P)).then_inc(max_loaded, 16)
            for k in range(len(passes)):
                feed(k)

        @block.gpsimd
        def _(pool):
            pool.iota(COL[:, :], [[1, P]], base=0, channel_multiplier=0, allow_small_or_imprecise_dtypes=True).then_inc(consts_ready, 1)
            pool.iota(TBASE[:, :], [[P, TILES]], base=0, channel_multiplier=0, allow_small_or_imprecise_dtypes=True).then_inc(consts_ready, 1)
            pool.iota(NODE[:, :], [[P, TILES]], base=0, channel_multiplier=1, allow_small_or_imprecise_dtypes=True).then_inc(consts_ready, 1)
            pool.iota(BEHIND[:, :], [[1, 1]], base=TB, channel_multiplier=TB, allow_small_or_imprecise_dtypes=True).then_inc(consts_ready, 1)
            pool.memset(IDENT[:, :], 0.0).then_inc(consts_ready, 1)
            pool.wait_ge(consts_ready, 5)
            pool.affine_select(out=IDENT[:, :], in_=IDENT[:, :], compare_op=ALU.not_equal, fill=1.0, base=0,
                               pattern=[[-1, P]], channel_multiplier=1).then_inc(consts_ready, 1)
            pool.wait_ge(span_in, 1)
            pool.iota(big[:, 0:GROUPS], [[1, GROUPS]], base=0, channel_multiplier=0, allow_small_or_imprecise_dtypes=True).then_inc(group_numbers, 1)
            pool.partition_all_reduce(extreme[:, :, :].rearrange("p a g -> p (a g)"), extreme[:, :, :].rearrange("p a g -> p (a g)"),
                                      P, bass.bass_isa.ReduceOp.max).then_inc(span_red, 1)
            pool.wait_ge(range_in, 1)
            pool.partition_all_reduce(rangev[:, :], rangev[:, :], P, bass.bass_isa.ReduceOp.max).then_inc(range_red, 1)
            pool.wait_ge(branch_ready, 1)
            pool.wait_ge(table_done, 16 * PAIRS)
            with pool.If(wide(pool) > 0):
                with pool.Fori(0, GROUPS) as g:
                    pool.wait_ge(max_loaded, g * 32 + 32)
                    settle(pool)
                    for c in range(C):
                        pool.indirect_dma_start(passes[0]["buf"][:, 0, c, :], None, passes[0]["table"][:, :],
                                                bass.IndirectOffsetOnAxis(idx[:, 0, c:c + 1], 0)).then_inc(max_gathered, 16)
            for k, ps in enumerate(passes):
                pool.wait_ge(table_done, 16 * (PAIRS + k * BLOCKS))
                buf = ps["buf"]
                with pool.Fori(0, ROUNDS) as i:
                    for s in range(SLOTS):
                        pool.wait_ge(slots_free, i * SLOTS + (k * GROUPS + s + 1))
                        pool.wait_ge(idx_loaded[s], i * 16 + (k * ROUNDS * 16 + 16))
                        settle(pool)
                        for c in range(C):
                            pool.indirect_dma_start(buf[:, s, c, 0:ps["row"]], None, ps["table"][:, :],
                                                    bass.IndirectOffsetOnAxis(idx[:, s, c:c + 1], 0)).then_inc(gathered[s], 16)

        def dense_tensor(pe, k, b):
            ps = passes[k]
            if ps["name"] in ("dev", "sage2", "sage4"):
                return
            pe.wait_ge(step_sem["stack_ready"], block_count("stack_ready", ps["name"], b))
            settle(pe)
            if ps["name"] == "gat":
                for j in range(2 * TB):
                    last = pe.transpose(ps_turn[:, j * P:(j + 1) * P], big[:, j * P:(j + 1) * P], IDENT[:, :])
                last.then_inc(step_sem["turned"], 1)
                return
            kdim = 2 * LAT if ps["name"] == "sage3" else 2 * D
            for j in range(TB):
                last = pe.transpose(ps_turn[0:kdim, j * P:(j + 1) * P], big[:, j * kdim:(j + 1) * kdim], IDENT[:, :])
            last.then_inc(step_sem["turned"], 1)
            wa = {"gine": W1S, "sage1": S1, "sage3": S3}[ps["name"]]
            wb = {"gine": W2, "sage1": S2, "sage3": S4}[ps["name"]]
            m = {"gine": D, "sage1": 2 * LAT, "sage3": 2 * D}[ps["name"]]
            pe.wait_ge(step_sem["copied"], block_count("copied", ps["name"], b))
            for q in range(2):
                last = pe.matmul(ps_hid[:, 512 * q:512 * q + HALF], wa[:, :], bigT[0:kdim, q * HALF:(q + 1) * HALF], start=True, stop=True)
            last.then_inc(step_sem["hidden"], 1)
            pe.wait_ge(step_sem["relued"], block_count("relued", ps["name"], b))
            for j in range(TB):
                last = pe.matmul(ps_out[:, j * m:(j + 1) * m], hid[:, j * P:(j + 1) * P], wb[:, :], start=True, stop=True)
            last.then_inc(step_sem["product"], 1)

        def gat_product(pe, b):
            pe.wait_ge(step_sem["copied"], block_count("copied", "gat", b))
            settle(pe)
            pe.wait_ge(product_read, b + 1)
            settle(pe)
            for j in range(TB):
                for q in range(2):
                    last = pe.matmul(ps_gat[:, j * D:(j + 1) * D], bigT[:, (2 * j + q) * P:(2 * j + q + 1) * P], MST[:, q, :],
                                     start=(q == 0), stop=(q == 1))
            last.then_inc(step_sem["product"], 1)

        @block.tensor
        def _(pe):
            spans = [[pe.alloc_register(f"pe_lo{q}"), pe.alloc_register(f"pe_hi{q}")] for q in range(6)]
            rest, spread = pe.alloc_register("pe_rest"), pe.alloc_register("pe_spread")
            pe.wait_ge(loaded, N_CONST)
            pe.wait_ge(consts_ready, 6)
            I64 = IDENT[0:D, 0:D]
            pe.transpose(ps_turn[:, 0:D], W[:, 0:P], I64)
            pe.transpose(ps_turn[:, D:2 * D], W[:, P:2 * P], I64)
            pe.transpose(ps_turn[0:D, 2 * D:3 * D], We[:, :], I64)
            pe.transpose(ps_turn[:, 512:512 + HID], nat1[:, :], IDENT[:, :])
            pe.transpose(ps_turn[:, 640:640 + 2 * LAT], nat2[:, :], I64)
            pe.transpose(ps_turn[0:2 * LAT, 704:704 + HID], nat3[:, :], IDENT[:, :])
            pe.transpose(ps_turn[:, 832:832 + 2 * D], nat4[:, :], IDENT[:, :]).then_inc(prep_t, 1)
            pe.wait_ge(prep_done, 1)
            for k in range(2):
                pe.matmul(ps_turn[:, 1024 + 64 * k:1088 + 64 * k], BD[:, k, :], Wl[:, k, :], start=True, stop=True)
            pe.matmul(ps_turn[:, 1536:1536 + HID], WeT[:, :, :].rearrange("p a b -> p (a b)"), W1[:, :], start=True, stop=True)
            for k in range(2):
                last = pe.matmul(ps_agg[:, 0:D], biasb[:, k, :], Wl[:, k, :], start=(k == 0), stop=(k == 1))
            last.then_inc(prep_t, 1)

            pe.wait_ge(x_loaded, 16)
            pe.wait_ge(prep_done, 3)
            pe.matmul(ps_agg[:, 0:P], biasb[:, 0, :], IDENT[:, :], start=True, stop=True).then_inc(prep_t, 1)
            with pe.Fori(0, PAIRS) as b:
                pe.wait_ge(score_in, b + 1)
                settle(pe)
                for q in range(2):
                    for j in range(TB):
                        last = pe.transpose(ps_turn[0:D, q * 1024 + j * P:q * 1024 + (j + 1) * P],
                                            big[:, (q * TB + j) * D:(q * TB + j + 1) * D], IDENT[:, :])
                    last.then_inc(score_t, 1)
                for q in range(2):
                    pe.wait_ge(score_c, b * 2 + (q + 1))
                    for j in range(q * TB, (q + 1) * TB):
                        last = pe.matmul(ps_out[:, j * 2 * H:(j + 1) * 2 * H], bigT[0:D, j * P:(j + 1) * P], Wa[:, :], start=True, stop=True)
                last.then_inc(score_mm, 1)

            def pass_tensor(k):
                ps = passes[k]
                gat = ps["name"] == "gat"
                n, parts, buf = ps["n"], ps["parts"], ps["buf"]

                hots = [onehot[0], onehot[1], onehot_rest] if parts == 1 else [onehot_h[0], onehot_h[1], onehot_rest_h]

                def aggregate(hot, s, done):
                    sums = ps_sums[hot]
                    if gat:
                        upper = upper_halves([*(onehots[:, q, :] for q in range(2)), onehot_rest_flat][hot])
                        for c in range(C):
                            for q in range(3):
                                pe.matmul(sums[:, H * D:H * D + (H if q else H + 1)], upper[:, c * P:(c + 1) * P],
                                          upper_halves(wparts[:, s % 2, c, q, 0:H if q else H + 1]),
                                          start=(c == 0 and q == 0), stop=(c == C - 1 and q == 2))
                    for c in range(C):
                        for q in range(parts):
                            if gat:
                                lhs, rhs = hots[hot][:, c, :], msg[:, s % 2, c, :]
                            elif parts == 1:
                                lhs, rhs = hots[hot][:, c, :], buf[:, s, c, 0:n]
                            else:
                                lhs, rhs = hots[hot][:, c, :], buf[:, s, c, q * n:(q + 1) * n]
                            last = pe.matmul(sums[:, 0:H * D if gat else n], lhs, rhs, start=(c == 0 and q == 0), stop=(c == C - 1 and q == parts - 1))
                    last.then_inc(done, 1)

                def further_tile(prev):
                    pe.reg_add(rest, rest, 1)
                    count = pe.snap(rest, min_val=1, max_val=GROUPS * TILES)
                    pe.wait_ge(ps["rest_hot"], count)
                    settle(pe)
                    pe.wait_ge(ps["rest_acc"], count)
                    settle(pe)
                    aggregate(2, prev, ps["rest_agg"])

                def second_tile(prev, lo, hi):
                    with pe.If(lo + 1 < hi):
                        further_tile(prev)

                def further_tiles(prev, lo, hi):
                    with pe.If(lo + 2 < hi):
                        with pe.Fori(lo + 2, hi) as t:
                            further_tile(prev)

                def expand(g, lo, hi):
                    pe.wait_ge(logit_ready, g + 1)
                    pe.matmul(ps_exp_all[:, 0:C * 2 * H], ZERO[:, :], ZERO[:, 0:C * 2 * H], start=True, stop=False)
                    with pe.Fori(lo, hi) as t:
                        pe.reg_add(spread, spread, 1)
                        pe.wait_ge(nodehot_ready, pe.snap(spread, min_val=1, max_val=GROUPS * TILES))
                        for c in range(C):
                            for q in range(3):
                                last = pe.matmul(ps_exp[:, c, :], nodehot[:, c * P:(c + 1) * P],
                                                 VALS[:, bass.ds(t, 1), q, :].rearrange("p a k -> p (a k)"),
                                                 start=False, stop=False)
                        last.then_inc(expand_done, 1)
                    pe.matmul(ps_exp_all[:, 0:C * 2 * H], ZERO[:, :], ZERO[:, 0:C * 2 * H],
                              start=False, stop=True).then_inc(expand_open, 1)

                def one_round(i):
                    for s in range(SLOTS):
                        g = i * SLOTS + s
                        load_spans(pe, spans, s, g)
                        last = (s - 1) % SLOTS, *last_span(pe, spans, s)
                        second_tile(*last)
                        if gat:
                            expand(g + 1, *next_span(pe, spans, s))
                        further_tiles(*last)
                        if gat:
                            pe.wait_ge(messages_ready, g * 2 + 2)
                            settle(pe)
                            pe.wait_ge(ps["first_hot"], g + 2)
                        else:
                            pe.wait_ge(gathered[s], i * (16 * C) + (k * ROUNDS + 1) * 16 * C)
                        settle(pe)
                        if ps["name"] == "gine":
                            pe.wait_ge(edges_loaded[s], i * 16 + 16)
                            settle(pe)
                        if not gat:
                            pe.wait_ge(ps["first_hot"], g + 1)
                            settle(pe)
                            pe.wait_ge(ps["first_acc"], g + 1)
                            settle(pe)
                        aggregate(s % 2, s, ps["first_agg"])

                for reg, value in ((rest, 0), (spans[3][0], 0), (spans[3][1], 1)):
                    pe.reg_mov(reg, value)
                pe.wait_ge(pass_open, k + 1)
                if gat:
                    pe.reg_mov(spread, 0)
                    pe.sem_inc(expand_done, 1)
                    load_span(pe, spans[0], 0)
                    expand(0, *span(pe, spans[0]))
                pe.matmul(ps_agg[:, 0:n], ZERO[:, :], ZEROS[:, 0:n], start=True, stop=True).then_inc(ps["first_agg"], 1)

                def dense(b, late=None):
                    if late:
                        late()
                    dense_tensor(pe, k, b)

                def finish():
                    second_tile(SLOTS - 1, *span(pe, spans[3]))
                    further_tiles(SLOTS - 1, *span(pe, spans[3]))

                sweep(pe, one_round, finish, dense,
                      (lambda b: gat_product(pe, b)) if gat else None)

            pe.wait_ge(branch_ready, 1)
            with pe.If(wide(pe) > 0):
                with pe.Fori(0, GROUPS) as g:
                    pe.wait_ge(max_diag, g + 1)
                    for h in range(H):
                        last = pe.matmul(ps_turn[:, h * GE:(h + 1) * GE], max_ones, max_diags[:, h, :, :].rearrange("p c v -> p (c v)"),
                                         start=True, stop=True)
                    last.then_inc(max_spread, 1)
            for k in range(len(passes)):
                pass_tensor(k)

        @block.scalar
        def _(act):
            act.dma_start(dst_i, dst_r).then_inc(dst_loaded, 16)
            act.dma_start(X[:, :, :], x.rearrange("(t p) d -> p t d", p=P)).then_inc(x_loaded, 16)
            with act.Fori(0, PAIRS) as b:
                for q in range(2):
                    act.wait_ge(score_t, b * 2 + (q + 1))
                    act.activation(bigT[0:D, q * TB * P:(q + 1) * TB * P], ps_turn[0:D, q * 1024:q * 1024 + TB * P], ACT.Copy).then_inc(score_c, 1)
            act.wait_ge(self_in, 1)
            act.activation(WSELF[:, :, :], WSELF[:, :, :], ACT.Exp).then_inc(self_exp, 1)

            def one_round(i):
                for s in range(SLOTS):
                    act.wait_ge(logit_ready, i * SLOTS + (s + 2))
                    act.activation(wparts[:, s % 2, :, 0, 0:H], lg[:, 2, :, :], ACT.Exp).then_inc(weight_ready, 1)
                    g = i * SLOTS + s
                    act.wait_ge(passes[0]["first_hot"], g + 1)
                    settle(act)
                    act.wait_ge(hot_in, g + 1)
                    for c in range(C):
                        act.activation(distance[:, c * P:(c + 1) * P], COL[:, :], ACT.Abs, scale=-1.0,
                                       bias=dst_in[:, s % 2, c:c + 1]).then_inc(hot_distance, 1)
                    act.wait_ge(hot_distance, g * C + C)
                    act.activation(onehots[:, s % 2, :], distance, ACT.Relu, scale=-1.0, bias=ONE[:, :]).then_inc(passes[0]["first_hot"], 1)

            def dense_scalar(k, b):
                ps = passes[k]
                name = ps["name"]
                if name in ("gine", "sage1", "sage3"):
                    kdim = 2 * LAT if name == "sage3" else 2 * D
                    bias = {"gine": b1, "sage1": sb1, "sage3": sb3}[name]
                    act.wait_ge(step_sem["turned"], block_count("turned", ps["name"], b))
                    act.activation(bigT[0:kdim, 0:TB * P], ps_turn[0:kdim, 0:TB * P], ACT.Copy).then_inc(step_sem["copied"], 1)
                    act.wait_ge(step_sem["hidden"], block_count("hidden", ps["name"], b))
                    act.activation(hid.rearrange("p (q n) -> p q n", q=2),
                                   ps_hid.rearrange("p (q n) -> p q n", q=2)[:, :, 0:HALF], ACT.Relu,
                                   bias=bias[:, :]).then_inc(step_sem["relued"], 1)
                if name == "dev":
                    act.wait_ge(dev_in, b + 1)
                    act.activation(tmp[:, 1, 0:TB * D], tmp[:, 1, 0:TB * D], ACT.Sqrt).then_inc(dev_out, 1)
                if name in ("gat", "dev", "gine", "sage4"):
                    act.wait_ge(step_sem["var_ready"], block_count("var_ready", ps["name"], b))
                    act.activation(small[:, 2, 0:TB], small[:, 1, 0:TB], ACT.Sqrt).then_inc(step_sem["std_ready"], 1)
                act.wait_ge(rows_ready[k + 1], b + 1)
                if name == "sage4":
                    act.dma_start(out[bass.ds(b * (TB * P), TB * P), :].rearrange("(t p) d -> p t d", p=P),
                                  X[:, bass.ds(b * TB, TB), :]).then_inc(out_done, 16)
                    return
                nxt = passes[k + 1]
                source = X[:, bass.ds(b * TB, TB), :]
                if name in STORING:
                    source, cols = ps["rows"], nxt["row"] // 3
                    act.wait_ge(table_done, b * 16 + (PAIRS + k * BLOCKS) * 16)
                    settle(act)
                    for q in range(3):
                        act.activation(source[:, :, q * cols:(q + 1) * cols],
                                       upper_halves(parts_of(TB * cols)[q]).rearrange("p (t k) -> p t k", t=TB), ACT.Copy).then_inc(rows_cut, 1)
                    act.wait_ge(rows_cut, b * 3 + (STORING.index(name) * BLOCKS * 3 + 3))
                    act.sem_inc(rows_free, 1)
                act.dma_start(nxt["table_tiles"][:, bass.ds(b * TB, TB), :], source).then_inc(table_done, 16)

            def gat_copy(b, late):
                late()
                act.wait_ge(step_sem["turned"], block_count("turned", "gat", b))
                act.activation(bigT[:, :], ps_turn[:, 0:TB * H * D], ACT.Copy).then_inc(step_sem["copied"], 1)

            for k in range(len(passes)):
                if k == 0:
                    sweep(act, one_round, lambda: None, gat_copy, lambda b: dense_scalar(0, b))
                else:
                    with act.Fori(0, BLOCKS) as b:
                        dense_scalar(k, b)
            act.wait_ge(out_done, 16 * BLOCKS)

        def same(dst, src):
            return nc.vector.tensor_scalar(dst, src, 1.0, None, ALU.mult)

        def dense_vector(ve, step, k, split, b):
            ps = passes[k]
            name, acc = ps["name"], acc_of[k]

            def blocked(ap, b):
                return ap[:, bass.ds(b * TB, TB), :]

            def view(buf, cols):
                return buf.rearrange("p (t k) -> p t k", t=TB) if cols is None else buf[:, 0:TB * cols].rearrange("p (t k) -> p t k", t=TB)

            def bcast(ap, cols):
                return ap.unsqueeze(2).broadcast_to([P, TB, cols])

            def row(ap, cols=D):
                return ap.unsqueeze(1).broadcast_to([P, TB, cols])

            def layer_norm(b, y, dst):
                mean, var, std = small[:, 0, 0:TB], small[:, 1, 0:TB], small[:, 2, 0:TB]
                sq = view(tmp[:, 3, :], D)
                step(ve.tensor_reduce(mean, y, X_AXIS, ALU.add))
                step(ve.tensor_scalar(mean, mean, 1.0 / D, None, ALU.mult))
                step(ve.tensor_tensor(y, y, bcast(mean, D), ALU.subtract))
                step(ve.tensor_tensor(sq, y, y, ALU.mult))
                step(ve.tensor_reduce(var, sq, X_AXIS, ALU.add))
                step(ve.tensor_scalar(var, var, 1.0 / D, LN_EPS, ALU.mult, ALU.add))
                ve.sem_inc(step_sem["var_ready"], 1)
                ve.wait_ge(step_sem["std_ready"], block_count("std_ready", ps["name"], b))
                step(ve.reciprocal(std, std))
                step(ve.tensor_tensor(dst, y, bcast(std, D), ALU.mult))
                return 8

            def store_parts(cols):
                v = parts_of(TB * cols)
                for q in range(2):
                    step(ve.tensor_tensor(v[q + 1], v[q], upper_halves(v[q]), ALU.subtract))
                ve.sem_inc(rows_ready[k + 1], 1)

            if name in STORING:
                if name != "gat":
                    ve.wait_ge(rows_free, b + (STORING.index(name) * BLOCKS + 2))
            y = view(tmp[:, 0, :], D)
            a = blocked(acc, b)
            xb = blocked(X, b)
            if name == "gat":
                ve.wait_ge(step_sem["product"], block_count("product", ps["name"], b))
                step(ve.tensor_tensor(y, view(ps_gat, D), xb, ALU.add))
                ve.sem_inc(product_read, 1)
                step(ve.tensor_tensor(y, y, row(CV[:, :]), ALU.add))
                layer_norm(b, y, xb)
                both = view(big, 2 * D)
                if not isinstance(b, int):
                    ve.wait_ge(step_sem["turned"], block_count("turned", "gat", b) + 1)
                    settle(ve)
                step(same(both[:, :, 0:D], xb))
                step(ve.tensor_tensor(both[:, :, D:2 * D], xb, xb, ALU.mult))
                store_parts(2 * D)
            if name == "dev":
                r = RDEG[:, bass.ds(b * TB, TB)]
                many = small[:, 5, 0:TB]
                step(ve.tensor_scalar(many, DEG[:, bass.ds(b * TB, TB)], 1.0, None, ALU.is_gt))
                v = view(tmp[:, 1, :], D)
                step(ve.tensor_tensor(y, a[:, :, 0:D], bcast(r, D), ALU.mult))
                step(ve.tensor_tensor(y, y, y, ALU.mult))
                step(ve.tensor_tensor(v, a[:, :, D:2 * D], bcast(r, D), ALU.mult))
                step(ve.tensor_tensor(v, v, y, ALU.subtract))
                step(ve.tensor_scalar(v, v, 0.0, None, ALU.max))
                step(ve.tensor_scalar(y, v, 0.0, None, ALU.is_gt))
                step(ve.tensor_tensor(y, y, bcast(many, D), ALU.mult))
                step(ve.tensor_scalar(v, v, 1e-30, None, ALU.max))
                ve.sem_inc(dev_in, 1)
                ve.wait_ge(dev_out, b + 1)
                step(ve.tensor_tensor(v, v, y, ALU.mult))
                step(ve.tensor_tensor(y, v, xb, ALU.add))
                layer_norm(b, y, xb)
                ve.sem_inc(rows_ready[k + 1], 1)
            if name == "gine":
                stack = view(big, 2 * D)
                u = view(tmp[:, 2, :], D)
                step(ve.tensor_tensor(u, row(Web[:, :]), bcast(DEG[:, bass.ds(b * TB, TB)], D), ALU.mult))
                step(ve.tensor_tensor(u, u, a[:, :, 0:D], ALU.add))
                step(ve.scalar_tensor_tensor(stack[:, :, 0:D], xb, epsb[:, :], u, ALU.mult, ALU.add))
                step(same(stack[:, :, D:2 * D], a[:, :, D:2 * D]))
                ve.sem_inc(step_sem["stack_ready"], 1)
                ve.wait_ge(step_sem["product"], block_count("product", ps["name"], b))
                step(ve.tensor_tensor(y, view(ps_out, D), xb, ALU.add))
                step(ve.tensor_tensor(y, y, row(b2[:, :]), ALU.add))
                layer_norm(b, y, xb)
                step(same(view(big, D), xb))
                store_parts(D)
            if name == "sage1":
                stack = view(big, 2 * D)
                step(ve.tensor_tensor(stack[:, :, 0:D], a, bcast(RDEG[:, bass.ds(b * TB, TB)], D), ALU.mult))
                step(same(stack[:, :, D:2 * D], xb))
                ve.sem_inc(step_sem["stack_ready"], 1)
                ve.wait_ge(step_sem["product"], block_count("product", ps["name"], b))
                prod = view(ps_out, 2 * LAT)
                pv = view(big, LAT)
                step(ve.tensor_copy(pv, prod[:, :, 0:LAT]))
                step(ve.tensor_tensor(blocked(Q2, b), prod[:, :, LAT:2 * LAT], row(sb2[:, :], LAT), ALU.add))
                store_parts(LAT)
            if name == "sage2":
                zb = blocked(Z, b)
                pv = view(big, LAT)
                step(ve.tensor_tensor(zb, a, bcast(RDEG[:, bass.ds(b * TB, TB)], LAT), ALU.mult))
                step(ve.tensor_tensor(zb, zb, blocked(Q2, b), ALU.add))
                step(same(pv, zb))
                store_parts(LAT)
            if name == "sage3":
                stack = view(big, 2 * LAT)
                step(ve.tensor_tensor(stack[:, :, 0:LAT], a, bcast(RDEG[:, bass.ds(b * TB, TB)], LAT), ALU.mult))
                step(same(stack[:, :, LAT:2 * LAT], blocked(Z, b)))
                ve.sem_inc(step_sem["stack_ready"], 1)
                ve.wait_ge(step_sem["product"], block_count("product", ps["name"], b))
                prod = view(ps_out, 2 * D)
                step(ve.tensor_copy(view(big, D), prod[:, :, 0:D]))
                step(ve.tensor_tensor(blocked(Q4, b), prod[:, :, D:2 * D], row(sb4[:, :]), ALU.add))
                store_parts(D)
            if name == "sage4":
                step(ve.tensor_tensor(y, a, bcast(RDEG[:, bass.ds(b * TB, TB)], D), ALU.mult))
                step(ve.tensor_tensor(y, y, blocked(Q4, b), ALU.add))
                step(ve.tensor_tensor(y, y, xb, ALU.add))
                layer_norm(b, y, xb)
                ve.sem_inc(rows_ready[k + 1], 1)

        def gat_normalise(ve, step, b):
            a = acc_of[0][:, bass.ds(b * TB, TB), :]
            ve.wait_ge(rows_free, b + 1)
            deg, rdeg = DEG[:, bass.ds(b * TB, TB)], RDEG[:, bass.ds(b * TB, TB)]
            step(same(deg, a[:, :, GATW - 1]))
            step(ve.tensor_scalar(small[:, 5, 0:TB], deg, 1.0, None, ALU.max))
            step(ve.reciprocal(small[:, 5, 0:TB], small[:, 5, 0:TB]))
            step(same(rdeg, small[:, 5, 0:TB]))
            sums = a[:, :, 0:H * D].rearrange("p t (h d) -> p t h d", h=H)
            b4 = big[:, :].rearrange("p (t h d) -> p t h d", t=TB, h=H)
            dd = small[:, 6, 0:TB * H].rearrange("p (t h) -> p t h", t=TB)
            step(ve.tensor_scalar(dd, a[:, :, H * D:H * D + H], 1e-16, None, ALU.add))
            step(ve.reciprocal(dd, dd))
            step(ve.tensor_tensor(b4, sums, dd.unsqueeze(3).broadcast_to([P, TB, H, D]), ALU.mult))
            ve.sem_inc(step_sem["stack_ready"], 1)

        @block.vector
        def _(ve):
            step, late_step = Chain(ve, chain_sem), Chain(ve, late_chain_sem)
            LATE_STEPS = 14
            ve.sem_inc(late_chain_sem, LATE_STEPS)
            spans = [[ve.alloc_register(f"ve_lo{q}"), ve.alloc_register(f"ve_hi{q}")] for q in range(6)]
            rest, spread = ve.alloc_register("ve_rest"), ve.alloc_register("ve_spread")

            step(ve.memset(ZEROS[:, :], 0.0))
            step(ve.memset(ONE[:, :], 1.0))
            step(ve.memset(BD[:, :, :], 0.0))
            step(ve.memset(wparts[:, :, :, :, H:H + 1], 1.0))
            step(ve.memset(DST[:, 0:C], -1.0))
            ve.wait_ge(dst_loaded, 16)
            step(ve.tensor_copy(DST[:, C:], dst_i))
            dst3 = DST[:, C:].rearrange("p (g c) -> p g c", c=C)
            step(ve.tensor_reduce(extreme[:, 0, :], dst3, X_AXIS, ALU.min))
            step(ve.tensor_scalar(extreme[:, 0, :], extreme[:, 0, :], -1.0, None, ALU.mult))
            step(ve.tensor_reduce(extreme[:, 1, :], dst3, X_AXIS, ALU.max))
            ve.sem_inc(span_in, 1)

            ve.wait_ge(loaded, N_CONST)
            ve.wait_ge(consts_ready, 6)
            for q in range(2):
                step(ve.tensor_tensor(att[:, q, :], att[:, q, :], W[:, :], ALU.mult))
                step(ve.tensor_reduce(Wa[:, q * H:(q + 1) * H], att[:, q, :].rearrange("p (h d) -> p h d", h=H), X_AXIS, ALU.add))
            ve.wait_ge(prep_t, 1)
            for k in range(2):
                step(ve.tensor_copy(BD[0:D, k, 0:D], ps_turn[0:D, k * D:(k + 1) * D]))
                step(ve.tensor_copy(BD[D:P, k, D:P], ps_turn[D:P, k * D:(k + 1) * D]))
                step(ve.tensor_copy(biasb[:, k, :], biasc[:, k:k + 1].broadcast_to([P, P])))
            step(ve.tensor_copy(WeT[:, 0, :], IDENT[0:D, 0:D]))
            step(ve.tensor_copy(WeT[:, 1, :], ps_turn[0:D, 2 * D:3 * D]))
            step(ve.tensor_copy(S1[:, :], ps_turn[:, 512:512 + HID]))
            step(ve.tensor_copy(S2[:, :], ps_turn[:, 640:640 + 2 * LAT]))
            step(ve.tensor_copy(S3[:, :], ps_turn[0:2 * LAT, 704:704 + HID]))
            step(ve.tensor_copy(S4[:, :], ps_turn[:, 832:832 + 2 * D]))
            ve.sem_inc(prep_done, 1)
            ve.wait_ge(prep_t, 2)
            step(ve.tensor_copy(MST[:, :, :], ps_turn[:, 1024:1024 + 2 * D].rearrange("p (k d) -> p k d", k=2)))
            step(ve.tensor_copy(W1S[:, :], ps_turn[:, 1536:1536 + HID]))
            step(ve.tensor_tensor(CV[:, :], ps_agg[:, 0:D], bl[:, :], ALU.add))
            ve.sem_inc(prep_done, 1)

            ve.wait_ge(span_red, 1)
            ve.wait_ge(group_numbers, 1)
            step(ve.tensor_scalar(extreme[:, 0, :], extreme[:, 0, :], -1.0, None, ALU.mult))
            for q in range(2):
                step(ve.tensor_copy(SPAN[:, 0:GROUPS, q], extreme[:, q, :]))
            step(ve.tensor_scalar(SPAN[:, 0:GROUPS, :], SPAN[:, 0:GROUPS, :], int(math.log2(P)), None, ALU.arith_shift_right))
            step(ve.tensor_copy(extreme[:, 1, :], SPAN[:, 0:GROUPS, 1]))
            step(ve.tensor_scalar(SPAN[:, 0:GROUPS, 1], extreme[:, 1, :], 1.0, None, ALU.add))
            step(ve.tensor_copy(extreme[:, 0, :], SPAN[:, 0:GROUPS, 0]))
            need = small[:, 0, 0:BLOCKS]
            step(ve.tensor_scalar(extreme[:, 1, :], extreme[:, 0, :], BEHIND[:, 0:1], None, ALU.is_lt))
            step(ve.tensor_tensor(extreme[:, 1, :], extreme[:, 1, :], big[:, 0:GROUPS], ALU.mult))
            step(ve.tensor_reduce(small[:, 1, 0:1], extreme[:, 1, :], X_AXIS, ALU.max))
            step(ve.tensor_copy(biasb[:, 0, :], small[:, 1, 0:1].broadcast_to([P, P])))
            ve.sem_inc(prep_done, 1)
            ve.wait_ge(prep_t, 3)
            step(ve.tensor_copy(need, ps_agg[:, 0:BLOCKS]))
            sched_i = SCHED[:, 1:BLOCKS + 1]
            step(ve.tensor_scalar(need, need, float(1 + SLOTS), None, ALU.add))
            step(ve.tensor_copy(sched_i, need))
            step(ve.tensor_scalar(sched_i, sched_i, int(math.log2(SLOTS)), None, ALU.arith_shift_right))
            step(ve.tensor_copy(need, sched_i))
            step(ve.tensor_scalar(small[:, 1, 0:BLOCKS], need, ROUNDS + 0.5, None, ALU.is_lt))
            step(ve.tensor_reduce(small[:, 2, 0:1], small[:, 1, 0:BLOCKS], X_AXIS, ALU.add))
            step(ve.tensor_copy(SCHED[:, BLOCKS + 1:BLOCKS + 2], small[:, 2, 0:1]))
            step(ve.tensor_scalar(need, need, float(ROUNDS), None, ALU.min))
            step(ve.tensor_copy(sched_i, need))
            step(ve.memset(SCHED[:, 0:1], 0))
            step(ve.memset(SPAN[:, GROUPS:GROUPS + 1, 0:1], TILES - 1))
            step(ve.memset(SPAN[:, GROUPS:GROUPS + 1, 1:2], TILES))

            ve.sem_inc(score_rows_free, 1)
            ve.wait_ge(x_loaded, 16)
            with ve.Fori(0, PAIRS) as b:
                step.loop(b, 4)
                pair = bass.ds(b * (2 * TB), 2 * TB)
                step(same(big[:, 0:2 * TB * D].rearrange("p (t d) -> p t d", t=2 * TB), X[:, pair, :]))
                ve.sem_inc(score_in, 1)
                ve.wait_ge(score_mm, b + 1)
                ve.wait_ge(score_rows_free, b + 1)
                scores = ps_out[:, 0:2 * TB * 2 * H].rearrange("p (t k) -> p t k", t=2 * TB)
                table = score_rows.rearrange("p (t k) -> p t k", t=2 * TB)
                step(same(ASRC[:, pair, :], scores))
                step(same(table[:, :, 0:D], X[:, pair, :]))
                step(ve.tensor_copy(table[:, :, D:GAT_ROW], scores[:, :, 0:H]))
                ve.sem_inc(score_m, 1)
            step.close(PAIRS)

            a_src, a_dst = ASRC[:, :, 0:H], ASRC[:, :, H:2 * H]
            by_head = a_src.rearrange("p t h -> p h t")
            step(ve.tensor_reduce(rangev[:, 0:H], by_head, X_AXIS, ALU.max))
            step(ve.tensor_reduce(rangev[:, H:2 * H], by_head, X_AXIS, ALU.min))
            step(ve.tensor_scalar(rangev[:, H:2 * H], rangev[:, H:2 * H], -1.0, None, ALU.mult))
            ve.sem_inc(range_in, 1)
            ve.wait_ge(range_red, 1)
            step(ve.tensor_copy(TOP, rangev[:, 0:H].unsqueeze(1).broadcast_to([P, TILES, H])))
            step(ve.tensor_tensor(rangev[:, H:2 * H], rangev[:, 0:H], rangev[:, H:2 * H], ALU.add))
            step(ve.tensor_reduce(rangev[:, 0:1], rangev[:, H:2 * H], X_AXIS, ALU.max))
            step(ve.tensor_scalar(rangev[:, 1:2], rangev[:, 0:1], SCORE_RANGE, None, ALU.is_gt))
            step(ve.tensor_copy(WIDE[:, :], rangev[:, 1:2]))
            ve.sem_inc(branch_ready, 1)
            with ve.If(wide(ve) > 0):
                slot = passes[0]["buf"][:, 0, :, D:D + H].rearrange("p c h -> p h c")
                ve.reg_mov(rest, 0)
                ve.memset(max_ones, 1.0).then_inc(max_step[3], 1)
                same(TOP, a_src).then_inc(max_step[3], 1)
                ve.wait_ge(max_step[3], 2)
                ve.sem_inc(max_free, 1)
                with ve.Fori(0, GROUPS) as g:
                    load_span(ve, spans[0], g)
                    lo, hi = span(ve, spans[0])
                    ve.wait_ge(max_gathered, g * (16 * C) + 16 * C)
                    settle(ve)
                    ve.tensor_tensor(max_diags, IDENT[:, :].unsqueeze(1).unsqueeze(1).broadcast_to([P, H, C, P]),
                                     slot.unsqueeze(3).broadcast_to([P, H, C, P]), ALU.mult).then_inc(max_diag, 1)
                    ve.wait_ge(max_spread, g + 1)
                    settle(ve)
                    with ve.Fori(lo, hi) as t:
                        ve.reg_add(rest, rest, 1)
                        done = ve.snap(rest, min_val=1, max_val=GROUPS * TILES)
                        ve.tensor_scalar(max_mask, dstb[:, 0, :], NODE[:, bass.ds(t, 1)], FAR, ALU.not_equal, ALU.mult).then_inc(max_step[0], 1)
                        ve.wait_ge(max_step[0], done)
                        ve.tensor_tensor(max_vals, ps_turn[:, :].rearrange("p (h e) -> p h e", h=H),
                                         max_mask.unsqueeze(1).broadcast_to([P, H, GE]), ALU.add).then_inc(max_step[1], 1)
                        ve.wait_ge(max_step[1], done)
                        ve.tensor_reduce(max_new, max_vals, X_AXIS, ALU.max).then_inc(max_step[2], 1)
                        ve.wait_ge(max_step[2], done)
                        ve.tensor_tensor(TOP[:, bass.ds(t, 1), :], TOP[:, bass.ds(t, 1), :], max_new.unsqueeze(1), ALU.max).then_inc(max_step[3], 1)
                        ve.wait_ge(max_step[3], done + 2)
                        settle(ve)
                    ve.sem_inc(max_free, 1)
            v8 = big[:, 0:TILES * 2 * H].rearrange("p (t k) -> p t k", t=TILES)
            t8 = big[:, 1024:1024 + TILES * 2 * H // 2].rearrange("p (t k) -> p t k", t=TILES)
            step(ve.tensor_copy(v8[:, :, 0:H], a_dst))
            step(ve.tensor_tensor(t8, a_dst, TOP, ALU.add))
            step(ve.tensor_scalar(v8[:, :, H:2 * H], t8, NEG_SLOPE, None, ALU.mult))
            step(ve.tensor_tensor(t8, t8, v8[:, :, H:2 * H], ALU.max))
            step(ve.tensor_scalar(v8[:, :, H:2 * H], t8, -1.0, None, ALU.mult))
            step(ve.tensor_tensor(WSELF[:, :, :], a_src, a_dst, ALU.add))
            step(ve.tensor_scalar(t8, WSELF[:, :, :], NEG_SLOPE, None, ALU.mult))
            step(ve.tensor_tensor(WSELF[:, :, :], WSELF[:, :, :], t8, ALU.max))
            step(ve.tensor_tensor(WSELF[:, :, :], WSELF[:, :, :], v8[:, :, H:2 * H], ALU.add))
            ve.sem_inc(self_in, 1)

            def split(value, dst, part_axis):
                for q in range(3):
                    step(ve.tensor_copy(part_axis(dst, q), value))
                    if q < 2:
                        step(ve.tensor_tensor(value, value, part_axis(dst, q), ALU.subtract))

            split(v8, VALS, lambda d, q: d[:, :, q, :])
            ve.wait_ge(self_exp, 1)

            ve.sem_inc(slots_free, SLOTS - 1)
            ve.sem_inc(rows_free, 2)
            ve.sem_inc(product_read, 1)
            ve.sem_inc(dstb_free, 2)

            def pass_vector(k):
                ps = passes[k]
                name, n, buf = ps["name"], ps["n"], ps["buf"]
                gat = name == "gat"
                acc = acc_of[k]
                oh = [*onehot, onehot_rest] if ps["parts"] == 1 else [*onehot_h, onehot_rest_h]

                def hot(q, cols, t):
                    return ve.scalar_tensor_tensor(oh[q], DST[:, bass.ds(cols, C)].unsqueeze(2).broadcast_to([P, C, P]),
                                                   TBASE[:, bass.ds(t, 1)], COL[:, :].unsqueeze(1).broadcast_to([P, C, P]),
                                                   ALU.subtract, ALU.is_equal)

                def add(t, q):
                    a = acc[:, bass.ds(t, 1), :]
                    return ve.tensor_tensor(a, a, ps_sums[q][:, 0:n].unsqueeze(1), ALU.add)

                def rest_begin(g, lo, hi):
                    with ve.If(lo + 1 < hi):
                        hot(2, g * C, nc.s_assert_within(lo + 1, 1, TILES - 1, skip_runtime_bounds_check_because="lo + 1 < hi")).then_inc(ps["rest_hot"], 1)

                def sum_last(s, g, lo, hi, frees=True):
                    ve.wait_ge(ps["first_acc"], g + 1)
                    settle(ve)
                    ve.wait_ge(ps["first_agg"], g + 1)
                    add(lo, (s - 1) % 2).then_inc(ps["first_acc"], 1)
                    with ve.If(lo + 1 < hi):
                        with ve.Fori(lo + 1, hi) as t:
                            ve.reg_add(rest, rest, 1)
                            count = ve.snap(rest, min_val=1, max_val=GROUPS * TILES)
                            ve.wait_ge(ps["rest_agg"], count)
                            add(t, 2).then_inc(ps["rest_acc"], 1)
                            ve.wait_ge(ps["rest_acc"], count + 1)
                            settle(ve)
                            with ve.If(t + 1 < hi):
                                hot(2, g * C, nc.s_assert_within(t + 1, 1, TILES - 1, skip_runtime_bounds_check_because="t + 1 < hi")).then_inc(ps["rest_hot"], 1)
                    if frees:
                        ve.sem_inc(slots_free, 1)

                def spread_dst(i, s, lo, hi):
                    ve.wait_ge(dstb_loaded[s % 2], i * (SLOTS // 2 * 16) + (16 * (s // 2) + 16))
                    settle(ve)
                    with ve.Fori(lo, hi) as t:
                        ve.wait_ge(expand_done, ve.snap(spread, min_val=1, max_val=GROUPS * TILES + 1))
                        ve.tensor_scalar(nodehot[:, :], dstb[:, s % 2, :], NODE[:, bass.ds(t, 1)], None, ALU.is_equal).then_inc(nodehot_ready, 1)
                        ve.reg_add(spread, spread, 1)

                def one_round(i):
                    for s in range(SLOTS):
                        g = i * SLOTS + s
                        load_spans(ve, spans, s, g)
                        lo, _ = this_span(ve, spans, s)
                        if not gat:
                            hot(s % 2, g * C + C, lo).then_inc(ps["first_hot"], 1)
                            rest_begin(g, *last_span(ve, spans, s))
                            sum_last(s, g, *last_span(ve, spans, s))
                            continue
                        weights = [wparts[:, s % 2, :, q, 0:H] for q in range(3)]
                        ve.wait_ge(expand_open, g + 1)
                        ve.sem_inc(dstb_free, 1)
                        ve.wait_ge(gathered[s], i * (16 * C) + (k * ROUNDS + 1) * 16 * C)
                        ve.tensor_tensor(lg[:, 0, :, :], ps_exp[:, :, 0:H], buf[:, s, :, D:D + H], ALU.add).then_inc(score_sum, 1)
                        ve.tensor_scalar(dst_in[:, s % 2, :], DST[:, bass.ds(g * C + C, C)], TBASE[:, bass.ds(lo, 1)], None, ALU.subtract).then_inc(hot_in, 1)
                        ve.wait_ge(score_sum, g + 1)
                        ve.scalar_tensor_tensor(lg[:, 1, :, :], lg[:, 0, :, :], NEG_SLOPE, lg[:, 0, :, :], ALU.mult, ALU.max).then_inc(score_leaky, 1)
                        ve.wait_ge(score_leaky, g + 1)
                        ve.tensor_tensor(lg[:, 2, :, :], lg[:, 1, :, :], ps_exp[:, :, H:2 * H], ALU.add).then_inc(logit_ready, 1)
                        rest_begin(g, *last_span(ve, spans, s))
                        spread_dst(i, s + 1, *next_span(ve, spans, s))
                        ve.wait_ge(weight_ready, g + 1)
                        ve.tensor_tensor(weights[1], weights[0], upper_halves(weights[0]), ALU.subtract).then_inc(weight_rest, 1)
                        ve.tensor_tensor(msg[:, s % 2, :, :].rearrange("p c (h d) -> p c h d", h=H),
                                         buf[:, s, :, 0:D].unsqueeze(2).broadcast_to([P, C, H, D]),
                                         weights[0].unsqueeze(3).broadcast_to([P, C, H, D]), ALU.mult).then_inc(messages_ready, 1)
                        ve.wait_ge(ps["first_acc"], g + 1)
                        settle(ve)
                        ve.wait_ge(weight_rest, g + 1)
                        ve.tensor_tensor(weights[2], weights[1], upper_halves(weights[1]), ALU.subtract).then_inc(messages_ready, 1)
                        sum_last(s, g, *last_span(ve, spans, s))
                    ve.wait_ge(ps["first_acc"], i * SLOTS + (SLOTS + 1))
                    settle(ve)

                def finish():
                    rest_begin(GROUPS, *span(ve, spans[3]))
                    sum_last(0, GROUPS, *span(ve, spans[3]), frees=False)
                    ve.wait_ge(ps["first_acc"], GROUPS + 2)
                    settle(ve)

                if gat:
                    step(ve.tensor_tensor(acc[:, :, 0:H * D].rearrange("p t (h d) -> p t h d", h=H),
                                          X[:, :, :].unsqueeze(2).broadcast_to([P, TILES, H, D]),
                                          WSELF[:, :, :].unsqueeze(3).broadcast_to([P, TILES, H, D]), ALU.mult))
                    step(ve.tensor_copy(acc[:, :, H * D:H * D + H], WSELF[:, :, :]))
                    step(ve.memset(acc[:, :, GATW - 1:GATW], 0.0))
                else:
                    step(ve.memset(ACC[:, 0:TILES * n], 0.0))
                for reg, value in ((rest, 0), (spans[3][0], 0), (spans[3][1], 1)):
                    ve.reg_mov(reg, value)
                if gat:
                    ve.reg_mov(spread, 1)
                    ve.wait_ge(score_rows_free, PAIRS + 1)
                    settle(ve)
                    ve.sem_inc(logit_ready, 1)
                    ve.sem_inc(ps["first_hot"], 1)
                if name == "gine":
                    step(ve.tensor_scalar(epsb[:, :], epsb[:, :], 1.0, None, ALU.add))
                ve.sem_inc(ps["first_acc"], 1)
                ve.sem_inc(ps["rest_acc"], 1)
                ve.sem_inc(pass_open, 1)
                if gat:
                    load_span(ve, spans[0], 0)
                    spread_dst(0, 0, *span(ve, spans[0]))
                per = {"gat": 7, "dev": 19, "gine": 17, "sage1": 6, "sage2": 5, "sage3": 6, "sage4": 11}[name]

                def dense(b, late_half=None):
                    step.loop(b, per)
                    if gat:
                        gat_normalise(ve, step, b)
                        late_half()
                    else:
                        dense_vector(ve, step, k, split, b)

                def late(b):
                    late_step.start(b, LATE_STEPS)
                    dense_vector(ve, late_step, k, split, b)
                    assert late_step.n == late_step.per

                sweep(ve, one_round, finish, dense, late if gat else None)
                step.close(BLOCKS)

            for k in range(len(passes)):
                pass_vector(k)


WEIGHTS = ["L0_gnn_W", "L0_gnn_att_src", "L0_gnn_att_dst", "L0_gnn_bias", "L0_gnn_Wl", "L0_gnn_bl",
           "L2_gnn_We_w", "L2_gnn_We_b", "L2_gnn_eps", "L2_gnn_W1", "L2_gnn_b1", "L2_gnn_W2", "L2_gnn_b2",
           "L3_gnn_Wl1", "L3_gnn_bl1", "L3_gnn_Wr1", "L3_gnn_Wl2", "L3_gnn_bl2", "L3_gnn_Wr2",
           "L3_gnn_Wl3", "L3_gnn_bl3", "L3_gnn_Wr3", "L3_gnn_Wl4", "L3_gnn_bl4", "L3_gnn_Wr4"]


def kernel(**inputs):
    import numpy as np
    import concourse.bacc as bacc
    from concourse.bass_utils import run_bass_kernel_spmd

    nc = bacc.Bacc("TRN2", target_bir_lowering=False, num_devices=1)
    pad = GROUPS * GE - N_EDGES
    src = np.pad(np.asarray(inputs["src"]), (0, pad), constant_values=0).reshape(GROUPS, P, C)
    dst = np.pad(np.asarray(inputs["dst"]), (0, pad + GE), constant_values=NPAD - 1).reshape(GROUPS + 1, P, C)
    arrays = {
        "x": np.pad(np.asarray(inputs["x"]), ((0, NPAD - N_NODES), (0, 0))),
        "edge_attr": np.asarray(inputs["edge_attr_64"]),
        "src_r": np.ascontiguousarray(src.transpose(1, 0, 2)).reshape(P, GROUPS * C),
        "dst_r": np.ascontiguousarray(dst[:GROUPS].transpose(1, 0, 2)).reshape(P, GROUPS * C),
        "dst_b": np.ascontiguousarray(dst.transpose(0, 2, 1)).reshape(GROUPS + 1, GE),
    }
    for name in WEIGHTS:
        arrays[name] = np.asarray(inputs[name])
    aps = {name: nc.dram_tensor(name, a.shape, mybir.dt.from_np(a.dtype), kind="ExternalInput").ap()
           for name, a in arrays.items()}
    out = nc.dram_tensor("out", (NPAD, D), F32, kind="ExternalOutput").ap()
    build(nc, aps["x"], aps["edge_attr"], aps["src_r"], aps["dst_r"], aps["dst_b"], {n: aps[n] for n in WEIGHTS}, out)
    r = run_bass_kernel_spmd(nc, [arrays], core_ids=[0])
    return r.results[0]["out"][:N_NODES]
```
